# Optimizing a Trainium2 kernel written in Bass

```python
import numpy as np
import jax
import jax.numpy as jnp

def _softmax(x, axis=-1):
    return jax.nn.softmax(x, axis=axis)

def _gelu(x):
    return jax.nn.gelu(x, approximate=True)

def _silu(x):
    return jax.nn.silu(x)

def _sigmoid(x):
    return jax.nn.sigmoid(x)

def _layernorm(x, axis=-1, eps=1e-05):
    m = jnp.mean(x, axis=axis, keepdims=True)
    v = jnp.var(x, axis=axis, keepdims=True)
    return (x - m) / jnp.sqrt(v + eps)

def _scatter_add(tgt, idx, src, axis=0):
    return tgt.at[idx].add(src)

def _segment_sum(src, seg, n):
    return jax.ops.segment_sum(src, seg, n)
kernel_name = 'mk_adaln_d1_jaxref_r8_377d10'

def setup_inputs(seed: int=0):
    np.random.seed(seed)
    _w = jnp.asarray

    def _L0_attn_setup():
        import jax, jax.numpy as jnp
        import numpy as np
        B, T, C = (4, 512, 128)
        key = jax.random.key(seed)
        x = jax.random.normal(key, (B, T, C), dtype=jnp.float32)
        return {'x': x}
    _L0_attn_in = _L0_attn_setup()

    def _L0_ffn_setup():
        import jax, jax.numpy as jnp
        import numpy as np
        B, SEQ, D, E, F = (4, 128, 128, 8, 512)
        CAPACITY = 2
        key = jax.random.key(seed)
        ks = jax.random.split(key, 8)
        x = jax.random.normal(ks[0], (B, SEQ, D), jnp.float32)
        gate_weight = jax.random.normal(ks[1], (E, D), jnp.float32) * 0.006
        W1 = jax.random.normal(ks[2], (E, D, F), jnp.float32) * (1.0 / np.sqrt(D))
        b1 = jnp.zeros((E, F), jnp.float32)
        W2 = jax.random.normal(ks[3], (E, F, D), jnp.float32) * (1.0 / np.sqrt(F))
        b2 = jnp.zeros((E, D), jnp.float32)
        Ws1 = jax.random.normal(ks[4], (D, F), jnp.float32) * (1.0 / np.sqrt(D))
        bs1 = jnp.zeros((F,), jnp.float32)
        Ws2 = jax.random.normal(ks[5], (F, D), jnp.float32) * (1.0 / np.sqrt(F))
        bs2 = jnp.zeros((D,), jnp.float32)
        return {'x': x, 'gate_weight': gate_weight, 'W1': W1, 'b1': b1, 'W2': W2, 'b2': b2, 'Ws1': Ws1, 'bs1': bs1, 'Ws2': Ws2, 'bs2': bs2}
    _L0_ffn_in = _L0_ffn_setup()
    _L0_c = _w((lambda *s: np.random.randn(*s).astype(np.float32) * 0.05)(2, 128))
    _L0_wmod = _w((lambda *s: np.random.randn(*s).astype(np.float32) * 0.05)(128, 6 * 128) * 128 ** (-0.5))
    _d = {'L0_attn_x': _L0_attn_in['x'], 'L0_ffn_gate_weight': _L0_ffn_in['gate_weight'], 'L0_ffn_W1': _L0_ffn_in['W1'], 'L0_ffn_b1': _L0_ffn_in['b1'], 'L0_ffn_W2': _L0_ffn_in['W2'], 'L0_ffn_b2': _L0_ffn_in['b2'], 'L0_ffn_Ws1': _L0_ffn_in['Ws1'], 'L0_ffn_bs1': _L0_ffn_in['bs1'], 'L0_ffn_Ws2': _L0_ffn_in['Ws2'], 'L0_ffn_bs2': _L0_ffn_in['bs2'], 'L0_c': _L0_c, 'L0_wmod': _L0_wmod}
    _x0 = _d['L0_attn_x']
    _d['L0_attn_x'] = jax.random.normal(jax.random.fold_in(jax.random.key(seed), 1), (2, 2048, 128), dtype=_x0.dtype)
    del _x0
    return _d

def reference(L0_attn_x, L0_ffn_gate_weight, L0_ffn_W1, L0_ffn_b1, L0_ffn_W2, L0_ffn_b2, L0_ffn_Ws1, L0_ffn_bs1, L0_ffn_Ws2, L0_ffn_bs2, L0_c, L0_wmod):

    def _L0_attn_ref(x):
        import jax, jax.numpy as jnp
        import numpy as np
        B, T, C = (4, 512, 128)
        t = x.shape[1]
        tril = jnp.tril(jnp.ones((t, t), dtype=x.dtype))
        wei = jnp.where(tril == 0, -jnp.inf, jnp.zeros((t, t), dtype=x.dtype))
        wei = jax.nn.softmax(wei, axis=-1)
        out = jnp.einsum('ts,bsc->btc', wei, x)
        return out

    def _L0_ffn_ref(x, gate_weight, W1, b1, W2, b2, Ws1, bs1, Ws2, bs2):
        import jax, jax.numpy as jnp
        import numpy as np
        B, SEQ, D, E, F = (4, 128, 128, 8, 512)
        CAPACITY = 2
        Bb, s, Dd = x.shape
        Ee = gate_weight.shape[0]
        xf = x.reshape(-1, Dd)
        S = xf.shape[0]
        logits = xf @ gate_weight.T
        scores = jax.nn.softmax(logits, axis=-1).T
        k = S * CAPACITY
        vals, idx = jax.lax.top_k(scores.reshape(-1), k)
        eidx = idx // S
        tidx = idx % S
        gate = jnp.zeros((Ee, S), x.dtype).at[eidx, tidx].add(vals)
        h = jax.nn.gelu(jnp.einsum('sd,edf->esf', xf, W1) + b1[:, None, :], approximate=True)
        y = jnp.einsum('esf,efd->esd', h, W2) + b2[:, None, :]
        out = jnp.einsum('es,esd->sd', gate, y)
        shared = jax.nn.gelu(xf @ Ws1 + bs1, approximate=True) @ Ws2 + bs2
        out = out + shared
        return out.reshape(Bb, s, Dd)
    x = L0_attn_x
    mod = (_silu(L0_c) @ L0_wmod).reshape(L0_c.shape[0], 6, 1, -1)
    sa, ca, ga, sb, cb, gb = (mod[:, 0], mod[:, 1], mod[:, 2], mod[:, 3], mod[:, 4], mod[:, 5])
    ga = (2 * (ga >= 0) - 1) * jnp.maximum(jnp.abs(ga), 0.25)
    gb = (2 * (gb >= 0) - 1) * jnp.maximum(jnp.abs(gb), 0.25)
    h = _layernorm(x, axis=-1) * (1 + ca) + sa
    x = x + ga * _L0_attn_ref(h)
    h = _layernorm(x, axis=-1) * (1 + cb) + sb
    x = x + gb * _L0_ffn_ref(h, L0_ffn_gate_weight, L0_ffn_W1, L0_ffn_b1, L0_ffn_W2, L0_ffn_b2, L0_ffn_Ws1, L0_ffn_bs1, L0_ffn_Ws2, L0_ffn_bs2)
    return x

_drawn_inputs = setup_inputs


def setup_inputs(seed=0):
    import zlib

    import numpy as np

    out = dict(_drawn_inputs(seed))
    spreads = {'L0_ffn_b1': (0.0, 2.0),
     'L0_ffn_b2': (0.0, 0.8),
     'L0_ffn_bs1': (0.0, 0.515),
     'L0_ffn_bs2': (0.0, 0.34)}
    factors = {}
    for name, (base, spread) in spreads.items():
        noise = np.random.default_rng([zlib.crc32(name.encode()), seed]).standard_normal(out[name].shape)
        drawn = base * np.exp(spread * noise) if base else spread * noise
        out[name] = jnp.asarray(drawn.astype(out[name].dtype))
    for name, factor in factors.items():
        out[name] = (out[name] * factor).astype(out[name].dtype)
    return out
```

```python
from contextlib import ExitStack

import numpy as np

import concourse.bass as bass
from concourse import mybir

ALU = mybir.AluOpType
ACT = mybir.ActivationFunctionType
F32 = mybir.dt.float32
F32R = mybir.dt.float32r
I32 = mybir.dt.int32
AX_X = mybir.AxisListType.X

P = 128
D = 128
F = 512
E = 8
NC = F // P
S = 4096
SEQ = 2048
BLK = 512
NB = S // BLK
NT = BLK // P
TOPK = 2 * S
EPS = 1e-5

HEAD_STEPS = 14
UNIT0 = 38
RING = 6
NSTASH = 6
NGB = 4
TOPK_SLOT = 4 * (NB - 1) + HEAD_STEPS


class Lane:

    def __init__(self):
        self.items = []


class Marks:

    def __init__(self, new_sem):
        self.new_sem = new_sem
        self.sems = {}

    def raise_(self, name, n):
        if name not in self.sems:
            self.sems[name] = [self.new_sem("s_" + name), 0]
        s = self.sems[name]
        s[1] += n
        return name, s[1]


def adaln_moe(nc, x, gw, w1, b1, w2, b2, ws1, bs1, ws2, bs2, c_in, wmod, consts, inv, out):
    gates_dram = nc.dram_tensor("gates_scratch", [E, S], F32, kind="Internal").ap()

    with ExitStack() as ctx:
        def sb(name, shape, dt=F32):
            return ctx.enter_context(nc.sbuf_tensor(name, shape, dt))

        def ps(name):
            return ctx.enter_context(nc.psum_tensor(name, [P, BLK], F32))

        marks = Marks(lambda n: ctx.enter_context(nc.semaphore(n)))
        lanes = {k: Lane() for k in ("sync", "scalar", "vector", "gpsimd", "tensor")}

        def put(lane, fn, after=(), mark=None, n=1):
            m = marks.raise_(mark, n) if mark else None
            lanes[lane].items.append((tuple(a for a in after if a), fn, m, n))
            return m

        def dma(lane, dst, src, mark, after=()):
            return put(lane, lambda e: e.dma_start(dst, src), after, mark, 16)

        W1h, W1l = sb("W1h", [P, E + 1, F], F32R), sb("W1l", [P, E + 1, F], F32R)
        W2h, W2l = sb("W2h", [P, E + 1, NC, D], F32R), sb("W2l", [P, E + 1, NC, D], F32R)
        H2h, H2l = sb("H2h", [P, S], F32R), sb("H2l", [P, S], F32R)
        ACC = sb("ACC", [P, S])
        ACE = sb("ACE", [P, 2, BLK])
        GB = sb("GB", [P, NGB, BLK])
        HF = sb("HF", [P, 4, BLK])
        Hh, Hl = sb("Hh", [P, RING, BLK], F32R), sb("Hl", [P, RING, BLK], F32R)
        TMP = sb("TMP", [P, 2, BLK])
        OUT = sb("OUT", [P, 2, NT, P])
        R1 = sb("R1", [P, 8192])
        CST = sb("CST", [P, 3 * P])
        COL = sb("COL", [P, 64])
        SM = sb("SM", [P, 192])
        GWh, GWl = sb("GWh", [P, E], F32R), sb("GWl", [P, E], F32R)
        CNT = sb("CNT", [P, 2])
        TI = sb("TI", [P, 4], I32)

        IDENT, TRI, ONES = CST[:, 0:P], CST[:, P:2 * P], CST[:, 2 * P:3 * P]
        STASH = R1[:, 0:NSTASH * BLK].rearrange("p (k s) -> p k s", k=NSTASH)
        WS = R1[:, 3072:5120].rearrange("p (k s) -> p k s", k=2)
        X = R1[:, 0:1536].rearrange("p (k t c) -> p k t c", k=3, t=NT)
        XN = R1[:, 1536:2560].rearrange("p (k t c) -> p k t c", k=2, t=NT)
        XN2 = R1[:, 2560:3072].rearrange("p (t c) -> p t c", t=NT)
        WMOD = R1[:, 5120:5888]
        ROWS = R1[0:64, 5888:6016]
        LR = R1[0:E, 5120:5632]
        CT = R1[:, 6144:7168].rearrange("p (k s) -> p k s", k=2)
        MT = R1[:, 7168:7680]
        INV = GB[:, 0:2, :]
        H2F = R1[:, 7680:8192]
        tk = [R1[:, 6144 + 256 * i:6400 + 256 * i] for i in range(8)]

        UB = [ps("U0"), ps("U1")]
        YB = [ps("Y0"), ps("Y1")]
        RB = [ps("R0"), ps("R1b"), ps("R2")]
        LG = ps("LG")

        SIL = SM[:, 0:2]
        MOD = SM[:, 2:14]
        MODv = MOD.rearrange("p (h k) -> p h k", h=2)
        SGN = SM[:, 14:18].rearrange("p (h k) -> p h k", h=2)
        MX = SM[:, 18:22].rearrange("p (h k) -> p h k", h=2)
        GG = SM[:, 22:26].rearrange("p (h k) -> p h k", h=2)
        OP = SM[:, 26:30].rearrange("p (h k) -> p h k", h=2)
        CA = SM[:, 30:32]
        CB = SM[:, 32:34]
        GBS = SM[:, 34:36]
        NHALF = SM[:, 36:40]
        KR = SM[:, 40:41]
        ST = SM[:, 64:112].rearrange("p (k t s) -> p k t s", k=2, t=NT)
        MV = SM[:, 112:128].rearrange("p (k t s) -> p k t s", k=2, t=NT)
        VE = SM[:, 128:136].rearrange("p (k t) -> p k t", k=2)
        NM = SM[:, 184:192].rearrange("p (k t) -> p k t", k=2)
        RS = SM[:, 136:152].rearrange("p (k j t) -> p k j t", k=2, j=2)

        ld_cst = dma("sync", CST[:, :], consts, "ld_cst")
        b1r = b1.rearrange("e (c p) -> (e c) p", p=P)
        ld_rows = None
        for dst, src in ((ROWS[0:32, :], b1r), (ROWS[32:36, :], bs1.rearrange("(c p) -> c p", p=P)),
                         (ROWS[36:44, :], b2), (ROWS[44:45, :], bs2.rearrange("(a p) -> a p", a=1)),
                         (ROWS[45:47, :], c_in), (ROWS[47:55, :], gw)):
            ld_rows = dma("scalar", dst, src, "ld_rows")

        x_used = {}

        def load_x(b):
            src = x[b * BLK:(b + 1) * BLK, :].rearrange("(t p) c -> p t c", p=P)
            return dma("sync", X[:, b % 3, :, :], src, f"ld_x{b % 3}", [x_used.get(b - 3)])

        ld_x = {0: load_x(0)}
        ld_wmod = dma("scalar", WMOD, wmod, "ld_wmod")
        ld_x[1] = load_x(1)

        w_used = {}
        ld_w = {}

        def load_w(j):
            k = WORDER.index(j) % 2
            s1 = ws1 if j == E else w1[j]
            s2 = (ws2 if j == E else w2[j]).rearrange("(c p) d -> p c d", p=P)
            free = w_used.get(k, ())
            dma("sync", WS[:, k, 0:F], s1, f"ld_w{k}", free)
            ld_w[j] = dma("sync", WS[:, k, F:2 * F].rearrange("p (c d) -> p c d", c=NC), s2, f"ld_w{k}")

        WORDER = [E] + list(range(E))
        inv_used = {}
        ld_inv = {}

        def load_inv(b):
            q = b % 4
            src = inv[0, q * BLK:(q + 1) * BLK].partition_broadcast(P)
            ld_inv[b] = dma("sync", INV[:, b % 2, :], src, f"ld_inv{b % 2}", [inv_used.get(b - 2)])

        load_w(E)
        load_inv(0)
        load_inv(1)
        ld_x[2] = load_x(2)
        load_w(0)

        nhalf = put("gpsimd", lambda e: e.memset(NHALF, -0.5), mark="nhalf")

        HB = RB + YB
        bank_read = [None] * len(HB)
        in_head = [True]
        bank_next = [0]

        def take_bank():
            k = bank_next[0] % (len(HB) if in_head[0] else len(RB))
            bank_next[0] += 1
            return k, HB[k], bank_read[k]

        kb, bank, free = take_bank()
        m = put("tensor", lambda e, bank=bank: e.transpose(bank[:, 0:55], ROWS[0:55, :], IDENT[0:55, 0:55]),
                [ld_cst, ld_rows], "pe_cols")
        cols = put("vector", lambda e, bank=bank: e.tensor_copy(COL[:, 0:55], bank[:, 0:55]), [m], "v_cols")
        bank_read[kb] = cols
        B1, B2, GWC = COL[:, 0:36], COL[:, 36:45], COL[:, 47:55]
        sil = put("scalar", lambda e: e.activation(SIL, COL[:, 45:47], ACT.Silu), [cols], "a_sil")
        gwh = put("vector", lambda e: e.tensor_copy(GWh[:, :], GWC), [cols], "v_gw")
        gwl = put("vector", lambda e: e.tensor_tensor(GWl[:, :], GWC, GWh[:, :].bitcast(F32), ALU.subtract),
                  [gwh], "v_gw")
        kb, bank, free = take_bank()
        for j in range(6):
            m = put("tensor", lambda e, j=j, bank=bank: e.matmul(
                bank[:, 2 * j:2 * j + 2], WMOD[:, j * P:(j + 1) * P], SIL, start=True, stop=True),
                [sil, ld_wmod], "pe_mod")
        mod = put("vector", lambda e, bank=bank: e.tensor_copy(MOD, bank[:, 0:12]), [m], "v_mod")
        bank_read[kb] = mod
        sgn = put("vector", lambda e: e.tensor_scalar(SGN, MODv[:, :, 4:6], 0.0, 2.0, ALU.is_ge, ALU.mult),
                  [mod], "v_mod")
        pm = put("vector", lambda e: e.tensor_scalar(SGN, SGN, 1.0, None, ALU.subtract), [sgn], "v_mod")
        mxa = put("vector", lambda e: e.tensor_tensor(MX, SGN, MODv[:, :, 4:6], ALU.mult), [pm], "v_mod")
        onep = put("vector", lambda e: e.tensor_scalar(OP, MODv[:, :, 2:4], 1.0, None, ALU.add), [mod], "v_mod")
        gg = put("vector", lambda e: e.scalar_tensor_tensor(GG, MX, 0.25, SGN, ALU.max, ALU.mult), [mxa], "v_mod")
        ca = put("vector", lambda e: e.tensor_tensor(CA, GG[:, 0, :], OP[:, 0, :], ALU.mult), [gg, onep], "v_mod")
        cbm = put("vector", lambda e: e.tensor_tensor(CB, GG[:, 0, :], MODv[:, 0, 0:2], ALU.mult), [gg], "v_mod")
        modv = put("vector", lambda e: e.tensor_scalar(GBS, GG[:, 1, :], B2[:, 8:9], None, ALU.mult),
                   [gg], "v_mod")
        C1, SB2, GBV = OP[:, 1, :], MODv[:, 1, 0:2], GG[:, 1, :]

        w_ready = {}

        def split_w(j, part, act, low):
            k = WORDER.index(j) % 2
            src = WS[:, k, part * F:(part + 1) * F]
            hi = (W1h[:, j, :] if part == 0 else W2h[:, j, :, :].rearrange("p c d -> p (c d)"))
            lo = (W1l[:, j, :] if part == 0 else W2l[:, j, :, :].rearrange("p c d -> p (c d)"))
            if act == "scalar":
                h = put(act, lambda e: e.activation(hi, src, ACT.Copy), [ld_w[j]], "a_w")
            else:
                h = put(act, lambda e: e.tensor_copy(hi, src), [ld_w[j]], "v_w")
            low_m = put(low, lambda e: e.tensor_tensor(lo, src, hi.bitcast(F32), ALU.subtract), [h],
                        {"vector": "v_wl", "gpsimd": "g_wl"}[low])
            w_ready[j, part] = (h, low_m)
            w_used[k] = w_used.get(k, ()) if part else ()
            w_used[k] = w_used[k] + (h, low_m)

        hd = {}
        ct_last = {}
        st_used = {}
        h2_ready = {}
        acc_ready = {}
        lg_ready = [None]
        xn_used = {}
        misc = {}

        def stats(b, src, ready, tag):
            k = {"1": 0, "2": 1}[tag]
            m = None
            for t in range(NT):
                m = put("vector", lambda e, t=t: e.bn_stats(ST[:, k, t, :], src[:, t, :]),
                        [ready, st_used.get(("st", k))] if t == 0 else (), "v_st")
            for t in range(NT):
                a = put("vector", lambda e, t=t: e.bn_aggr(MV[:, k, t, :], ST[:, k, t, :]),
                        [m, st_used.get(("mv", k))] if t == 0 else (), "v_st")
            st_used["st", k] = a
            v = put("gpsimd", lambda e: e.tensor_scalar(VE[:, k, :], MV[:, k, :, 1], 1.0, EPS, ALU.mult, ALU.add),
                    [a], "g_rs")
            r = put("gpsimd", lambda e: e.tensor_tensor(RS[:, k, 0, :], VE[:, k, :], NHALF, ALU.pow),
                    [v, nhalf, st_used.get(("rs", k))], "g_rs")
            g = put("gpsimd", lambda e: e.tensor_scalar(NM[:, k, :], MV[:, k, :, 0], -1.0, 0.0, ALU.mult, ALU.add),
                    [a], "g_rs")
            n = put("gpsimd", lambda e: e.tensor_tensor(RS[:, k, 1, :], NM[:, k, :], RS[:, k, 0, :], ALU.mult),
                    [r, g], "g_rs")
            st_used["mv", k] = n
            return n

        def transposes(dst, src, after, mark):
            for t in range(NT):
                m = put("tensor", lambda e, t=t: e.transpose(dst(t), src(t), IDENT), after if t == 0 else (),
                        mark if t == NT - 1 else None)
            return m

        def head(b, s):
            n = b // 4
            q = hd.setdefault(b, {})
            xs = X[:, b % 3, :, :]
            if s == 0:
                q["nm"] = stats(b, xs, ld_x[b], "1")
            elif s == 2:
                for t in range(NT):
                    free = [q["nm"], xn_used.get(b - 2)]
                    if t < 3:
                        q["xn", "scalar"] = put("scalar", lambda e, t=t: e.activation(
                            XN[:, b % 2, t, :], xs[:, t, :], ACT.Identity, bias=RS[:, 0, 1, t:t + 1],
                            scale=RS[:, 0, 0, t:t + 1]), free, "a_xn")
                    else:
                        q["xn", "gpsimd"] = put("gpsimd", lambda e, t=t: e.tensor_scalar(
                            XN[:, b % 2, t, :], xs[:, t, :], RS[:, 0, 0, t:t + 1], RS[:, 0, 1, t:t + 1],
                            ALU.mult, ALU.add), free, "g_xn")
                st_used["rs", 0] = q["xn", "scalar"]
            elif s == 3:
                k1, T1, f1 = take_bank()
                q["t1"] = transposes(lambda t: T1[:, t * P:(t + 1) * P], lambda t: XN[:, b % 2, t, :],
                                     [q["xn", "scalar"], q["xn", "gpsimd"], f1], "pe_t1")
                k2, T2, f2 = take_bank()
                q["t2"] = transposes(lambda t: T2[:, t * P:(t + 1) * P], lambda t: xs[:, t, :], [f2], "pe_t2")
                xn_used[b] = q["t1"]
                x_used[b] = q["t2"]
                q["T1"], q["T2"] = (k1, T1), (k2, T2)
                if b + 3 < NB:
                    ld_x[b + 3] = load_x(b + 3)
            elif s == 4:
                k1, T1 = q["T1"]
                k2, T2 = q["T2"]
                first = b % 4 == 0
                init = 0.0 if first else CT[:, (b - 1) % 2, BLK - 1:BLK]
                c = put("vector", lambda e: e.tensor_tensor_scan(
                    CT[:, b % 2, :], ONES[:, 0:1].to_broadcast([P, BLK]), T1[:, :], init, ALU.mult, ALU.add),
                    [q["t1"], ct_last.get(b - 1), ld_cst], "v_ct")
                ct_last[b] = c
                bank_read[k1] = c
                mm = put("vector", lambda e: e.scalar_tensor_tensor(
                    MT, CT[:, b % 2, :], CA[:, n:n + 1], INV[:, b % 2, :], ALU.mult, ALU.mult),
                    [c, ld_inv[b], modv, misc.get("mt")], "v_mt")
                inv_used[b] = mm
                if b + 2 < NB:
                    load_inv(b + 2)
                q["x2"] = put("vector", lambda e: e.scalar_tensor_tensor(
                    ACC[:, b * BLK:(b + 1) * BLK], T2[:, :], CB[:, n:n + 1], MT, ALU.add, ALU.add),
                    [mm, q["t2"]], "v_x2")
                misc["mt"] = q["x2"]
                bank_read[k2] = q["x2"]
            elif s == 5:
                k3, T3, f3 = take_bank()
                q["t3"] = transposes(lambda t: T3[:, t * P:(t + 1) * P],
                                     lambda t: ACC[:, b * BLK + t * P:b * BLK + (t + 1) * P],
                                     [q["x2"], f3], "pe_t3")
                q["T3"] = (k3, T3)
                acc_ready[b] = q["t3"]
            elif s == 6:
                k3, T3 = q["T3"]
                q["nm2"] = stats(b, T3[:, :].rearrange("p (t c) -> p t c", t=NT), q["t3"], "2")
            elif s == 8:
                k3, T3 = q["T3"]
                for t in range(NT):
                    m = put("scalar", lambda e, t=t: e.activation(
                        XN2[:, t, :], T3[:, t * P:(t + 1) * P], ACT.Identity,
                        bias=RS[:, 1, 1, t:t + 1], scale=RS[:, 1, 0, t:t + 1]),
                        [q["nm2"], misc.get("xn2")], "a_xn2")
                q["xn2"] = m
                st_used["rs", 1] = m
                bank_read[k3] = m
            elif s == 9:
                k4, T4, f4 = take_bank()
                q["t4"] = transposes(lambda t: T4[:, t * P:(t + 1) * P], lambda t: XN2[:, t, :],
                                     [q["xn2"], f4], "pe_t4")
                misc["xn2"] = q["t4"]
                q["T4"] = (k4, T4)
            elif s == 10:
                k4, T4 = q["T4"]
                f = put("scalar", lambda e: e.activation(H2F, T4[:, :], ACT.Identity, bias=SB2[:, n:n + 1],
                                                         scale=C1[:, n:n + 1]),
                        [q["t4"], misc.get("h2l"), misc.get("h2h")], "a_h2f")
                bank_read[k4] = f
                h = put("scalar", lambda e: e.activation(H2h[:, b * BLK:(b + 1) * BLK], H2F, ACT.Copy), [f], "a_h2")
                q["h2h"] = h
            elif s == 11:
                h = q["h2h"]
                lo = put("vector", lambda e: e.tensor_tensor(
                    H2l[:, b * BLK:(b + 1) * BLK], H2F, H2h[:, b * BLK:(b + 1) * BLK].bitcast(F32), ALU.subtract),
                    [h], "v_h2l")
                misc["h2l"], misc["h2h"] = lo, h
                h2_ready[b] = (h, lo)
            elif s == 12:
                k5, T5, f5 = take_bank()
                hs, ls = H2h[:, b * BLK:(b + 1) * BLK], H2l[:, b * BLK:(b + 1) * BLK]
                for i, (a, r) in enumerate(((GWh, hs), (GWh, ls), (GWl, hs))):
                    m = put("tensor", lambda e, a=a, r=r, i=i: e.matmul(
                        T5[0:E, :], a[:, :], r, start=i == 0, stop=i == 2),
                        [*h2_ready[b], gwl, f5] if i == 0 else (), "pe_lr" if i == 2 else None)
                q["lr"], q["T5"] = m, (k5, T5)
            elif s == 13:
                k5, T5 = q["T5"]
                m = put("scalar", lambda e: e.activation(LR, T5[0:E, :], ACT.Copy),
                        [q["lr"], misc.get("lrt"), mod], "a_lr")
                bank_read[k5] = m
                for t in range(NT):
                    j = (b * NT + t) * E
                    mt = put("tensor", lambda e, t=t, j=j: e.transpose(
                        LG[:, j:j + E], LR[:, t * P:(t + 1) * P], IDENT[0:E, 0:E]), [m],
                        "pe_lg" if t == NT - 1 else None)
                misc["lrt"] = mt
                lg_ready[0] = mt

        units = [(E, b) for b in range(NB)] + [(j, b) for b in range(NB) for j in range(E)]
        gelu, cast, low, h_used = {}, {}, {}, {}
        u_read = [None, None]
        y_read = [None, None]
        y_done = {}

        def up(g):
            j, b = units[g // NC]
            c = g % NC
            bank = UB[g % 2]
            wh, wl = W1h[:, j, c * P:(c + 1) * P], W1l[:, j, c * P:(c + 1) * P]
            hs, ls = H2h[:, b * BLK:(b + 1) * BLK], H2l[:, b * BLK:(b + 1) * BLK]
            for i, (a, r) in enumerate(((wh, hs), (wh, ls), (wl, hs))):
                m = put("tensor", lambda e, a=a, r=r, i=i: e.matmul(bank[:, :], a, r, start=i == 0, stop=i == 2),
                        [*h2_ready[b], *w_ready[j, 0], u_read[g % 2]] if i == 0 else (), "pe_up" if i == 2 else None)
            bias = B1[:, j * NC + c:j * NC + c + 1]
            gelu[g] = put("scalar", lambda e: e.activation(HF[:, g % 4, :], bank[:, :], ACT.Gelu_apprx_tanh, bias=bias),
                          [m, low.get(g - 4), cast.get(g - 4), cols], "a_gelu")
            u_read[g % 2] = gelu[g]

        def cast_h(g):
            hi, lo, src = Hh[:, g % RING, :], Hl[:, g % RING, :], HF[:, g % 4, :]
            if g % NC == 1:
                cast[g] = put("vector", lambda e: e.tensor_copy(hi, src), [gelu[g], h_used.get(g - RING)], "v_cast")
            else:
                cast[g] = put("scalar", lambda e: e.activation(hi, src, ACT.Copy),
                              [gelu[g], h_used.get(g - RING)], "a_cast")

        def low_h(g):
            hi, lo, src = Hh[:, g % RING, :], Hl[:, g % RING, :], HF[:, g % 4, :]
            lane = "gpsimd" if g % NC == 3 and g < NC * NB else "vector"
            low[g] = put(lane, lambda e: e.tensor_tensor(lo, src, hi.bitcast(F32), ALU.subtract),
                         [cast[g], h_used.get(g - RING)], {"vector": "v_low", "gpsimd": "g_low"}[lane])

        def down(g):
            u = g // NC
            j, b = units[u]
            c = g % NC
            bank = YB[u % 2]
            wh, wl = W2h[:, j, c, :], W2l[:, j, c, :]
            hi, lo = Hh[:, g % RING, :], Hl[:, g % RING, :]
            for i, (a, r) in enumerate(((wh, hi), (wh, lo), (wl, hi))):
                m = put("tensor", lambda e, a=a, r=r, i=i: e.matmul(
                    bank[:, :], a, r, start=(c == 0 and i == 0), stop=(c == NC - 1 and i == 2)),
                    [cast[g], low[g], *w_ready[j, 1], y_read[u % 2] if c == 0 else None] if i == 0 else (),
                    "pe_dn" if i == 2 else None)
            h_used[g] = m
            if c == NC - 1:
                y_done[u] = m

        tmp_used = [None, None]
        tmp_next = [0]
        ace_last = {}
        ace_free = {}
        out_free = [None, None]
        stash_put = {}
        gb_ld = {}
        gb_used = {}
        jobs = [(j, b) for b in range(NB) for j in range(E)]
        g_written = [None]
        shared_done = {}
        stored = []

        def load_gb(i):
            if i < len(jobs):
                j, b = jobs[i]
                src = gates_dram[j, b * BLK:(b + 1) * BLK].partition_broadcast(P)
                gb_ld[i] = dma("sync", GB[:, i % NGB, :], src, f"ld_gb{i % NGB}", [*g_written[0], gb_used.get(i - NGB)])

        def take_tmp():
            k = tmp_next[0] % 2
            tmp_next[0] += 1
            return k

        def finish_shared(u):
            b = units[u][1]
            n = b // 4
            bank = YB[u % 2]
            k = take_tmp()
            a = put("scalar", lambda e: e.activation(TMP[:, k, :], bank[:, :], ACT.Identity,
                                                     bias=GBS[:, n:n + 1], scale=GBV[:, n:n + 1]),
                    [y_done[u], tmp_used[k], modv], "a_sh")
            y_read[u % 2] = a
            acc = ACC[:, b * BLK:(b + 1) * BLK]
            tmp_used[k] = shared_done[b] = put(
                "gpsimd", lambda e: e.tensor_tensor(acc, acc, TMP[:, k, :], ALU.add), [a, acc_ready[b]], "g_sh")

        def stash(u):
            j = units[u][0]
            bank = YB[u % 2]
            stash_put[u] = put("scalar", lambda e: e.activation(
                STASH[:, u - NB, :], bank[:, :], ACT.Identity, bias=B2[:, j:j + 1]),
                [y_done[u], *head_over], "a_stash")
            y_read[u % 2] = stash_put[u]

        def gate(u):
            i = u - NB
            j, b = jobs[i]
            k = take_tmp()
            last = i == len(jobs) - 1
            dst = ACE[:, b % 2, :] if j == 0 else TMP[:, k, :]
            free = ace_free.get(b - 2) if j == 0 else tmp_used[k]
            if u in stash_put:
                m = put("vector", lambda e: e.tensor_tensor(dst, STASH[:, i, :], GB[:, i % NGB, :], ALU.mult),
                        [stash_put[u], gb_ld[i], free], "v_gate")
            else:
                bank = YB[u % 2]
                m = put("vector", lambda e: e.scalar_tensor_tensor(
                    dst, bank[:, :], B2[:, j:j + 1], GB[:, i % NGB, :], ALU.add, ALU.mult),
                    [y_done[u], gb_ld[i], free], "v_gate")
                y_read[u % 2] = m
            gb_used[i] = m
            load_gb(i + NGB)
            if j == 0:
                ace_last[b] = m
            else:
                lane = "vector" if last else "gpsimd"
                a = ACE[:, b % 2, :]
                ace_last[b] = tmp_used[k] = put(
                    lane, lambda e: e.tensor_tensor(a, a, TMP[:, k, :], ALU.add), [m, ace_last[b]],
                    {"vector": "v_ace", "gpsimd": "g_ace"}[lane])

        fin = {}

        def close_a(b):
            n = b // 4
            acc = ACC[:, b * BLK:(b + 1) * BLK]
            ace_free[b] = fin[b] = put("vector", lambda e: e.scalar_tensor_tensor(
                acc, ACE[:, b % 2, :], GBV[:, n:n + 1], acc, ALU.mult, ALU.add),
                [ace_last[b], shared_done[b]], "v_fin")

        def close_b(b):
            k, bank, free = take_bank()
            m = transposes(lambda t: bank[:, t * P:(t + 1) * P],
                           lambda t: ACC[:, b * BLK + t * P:b * BLK + (t + 1) * P], [fin[b], free], "pe_out")
            o = put("scalar", lambda e: e.activation(OUT[:, b % 2, :, :].rearrange("p t c -> p (t c)"), bank[:, :],
                                                     ACT.Copy), [m, out_free[b % 2]], "a_out")
            bank_read[k] = o
            dst = out[b * BLK:(b + 1) * BLK, :].rearrange("(t p) c -> p t c", p=P)
            out_free[b % 2] = dma("sync", dst, OUT[:, b % 2, :, :], f"st_out{b % 2}", [o])
            stored.append(out_free[b % 2])

        SC, EX, GT, EQ, CUMX, RK, SEL, GG2 = tk
        SCv = SC.rearrange("p (e t) -> p e t", e=E)
        tkm = {}
        T_I, C_I, M_I = TI[:, 0:1], TI[:, 1:2], TI[:, 2:3]
        MXR, SMR, RCR = SM[:, 152:184], COL[:, 0:1], None
        RED = sb("RED", [P, 3, NB * NT])
        LGv = LG[:, 0:256].rearrange("p (t e) -> p t e", e=E)
        BITS = list(range(29, -1, -1))

        def tk_softmax(step):
            EXv = EX.rearrange("p (t e) -> p t e", e=E)
            if step == 0:
                a = put("vector", lambda e: e.tensor_reduce(RED[:, 0, :], LGv, AX_X, ALU.max), [lg_ready[0]], "v_tk")
                tkm["sub"] = put("vector", lambda e: e.tensor_tensor(
                    EXv, LGv, RED[:, 0, :].unsqueeze(2).to_broadcast([P, NB * NT, E]), ALU.subtract),
                    [a, *head_over], "v_tk")
                tkm["exp"] = put("scalar", lambda e: e.activation(EX, EX, ACT.Exp), [tkm["sub"]], "a_exp")
            else:
                a = put("vector", lambda e: e.tensor_reduce(RED[:, 1, :], EXv, AX_X, ALU.add), [tkm["exp"]], "v_tk")
                r = put("vector", lambda e: e.reciprocal(RED[:, 2, :], RED[:, 1, :]), [a], "v_tk")
                tkm["sc"] = put("vector", lambda e: e.tensor_tensor(
                    SCv.rearrange("p e t -> p t e"), EXv,
                    RED[:, 2, :].unsqueeze(2).to_broadcast([P, NB * NT, E]), ALU.mult), [r], "v_tk")
                z = put("vector", lambda e: e.memset(T_I, 0), mark="v_tk")
                tkm["t"] = z
                tkm["cand"] = put("vector", lambda e: e.memset(C_I, 1 << BITS[0]), mark="v_tk")

        def tk_count(i):
            tkm["cnt"] = put("vector", lambda e: e.tensor_scalar(
                GT, SC, C_I.bitcast(F32), None, ALU.is_ge, ALU.add, accum_out=CNT[:, i % 2:i % 2 + 1]),
                [tkm["sc"], tkm["cand"]], "v_cnt")

        def tk_sum(i):
            tkm["sum"] = put("tensor", lambda e: e.matmul(LG[:, 256 + i % 2:257 + i % 2], ONES,
                                                          CNT[:, i % 2:i % 2 + 1], start=True, stop=True),
                             [tkm["cnt"]], "pe_sum")

        def tk_step(i):
            bit = BITS[i]
            m = put("vector", lambda e: e.tensor_scalar(M_I, LG[:, 256 + i % 2:257 + i % 2], float(TOPK),
                                                        float(1 << bit), ALU.is_ge, ALU.mult),
                    [tkm["sum"], tkm["t"]], "v_tk")
            if bit:
                tkm["cand"] = put("vector", lambda e: e.scalar_tensor_tensor(
                    C_I, M_I, 1 << (bit - 1), T_I, ALU.bitwise_or, ALU.bitwise_or), [m, tkm["cnt"]], "v_cand")
            tkm["t"] = put("vector", lambda e: e.tensor_tensor(T_I, T_I, M_I, ALU.bitwise_or),
                           [m, tkm["t"], tkm["cand"]], "v_tk")

        def tk_ties(s):
            TF = T_I.bitcast(F32)
            if s == 0:
                a = put("vector", lambda e: e.tensor_scalar(GT, SC, TF, None, ALU.is_gt, ALU.add,
                                                            accum_out=CNT[:, 0:1]), [tkm["t"], tkm["cnt"]], "v_tk")
                q = put("vector", lambda e: e.tensor_scalar(EQ, SC, TF, None, ALU.is_equal), [tkm["t"]], "v_tk")
                tkm["masks"] = q
            elif s == 1:
                k, bank, free = take_bank()
                put("tensor", lambda e: e.matmul(LG[:, 260:261], ONES, CNT[:, 0:1], start=True, stop=True),
                    [tkm["masks"]])
                put("tensor", lambda e: e.matmul(bank[:, 0:256], TRI, EQ, start=True, stop=True), [free])
                m = put("tensor", lambda e: e.matmul(bank[:, 256:512], ONES, EQ, start=True, stop=True),
                        mark="pe_tie")
                r = put("vector", lambda e: e.tensor_scalar(KR, LG[:, 260:261], -1.0, float(TOPK), ALU.mult, ALU.add),
                        [m], "v_tk")
                c = put("vector", lambda e: e.tensor_tensor_scan(
                    CUMX, ONES[:, 0:1].to_broadcast([P, 256]), bank[:, 256:512], 0.0, ALU.mult, ALU.add), [m], "v_tk")
                c2 = put("vector", lambda e: e.tensor_tensor(RK, CUMX, bank[:, 256:512], ALU.subtract), [c], "v_tk")
                c3 = put("vector", lambda e: e.tensor_tensor(RK, RK, bank[:, 0:256], ALU.add), [c2], "v_tk")
                bank_read[k] = c3
                tkm["rk"] = c3
            elif s == 2:
                a = put("vector", lambda e: e.scalar_tensor_tensor(SEL, RK, KR, EQ, ALU.is_le, ALU.mult),
                        [tkm["rk"]], "v_tk")
                a = put("vector", lambda e: e.tensor_tensor(SEL, SEL, GT, ALU.add), [a], "v_tk")
                tkm["g"] = put("vector", lambda e: e.tensor_tensor(GG2, SEL, SC, ALU.mult), [a], "v_tk")
            elif s == 3:
                k, bank, free = take_bank()
                for h in range(2):
                    m = put("tensor", lambda e, h=h: e.transpose(bank[:, h * P:(h + 1) * P],
                                                                 GG2[:, h * P:(h + 1) * P], IDENT),
                            [tkm["g"], free] if h == 0 else (), "pe_gt" if h else None)
                c = put("scalar", lambda e: e.activation(RK, bank[:, 0:256], ACT.Copy), [m, tkm["g"]], "a_gt")
                bank_read[k] = c
                dst = gates_dram.rearrange("e (t p) -> (e t) p", p=P).rearrange("(k q) p -> q k p", q=P)
                g_written[0] = [dma("sync", dst, RK.rearrange("q (k p) -> q k p", k=2), "st_gates", [c])]
                for i in range(NGB):
                    load_gb(i)

        n_slots = UNIT0 + NC * len(units) + NC + 1
        head_over = []
        tie0 = TOPK_SLOT + 3 + len(BITS)
        split_w(E, 0, "scalar", "vector")
        gate_next = NB
        n_tie = 0
        pending = []
        for s in range(n_slots + 8):
            g = s - UNIT0
            if s == UNIT0:
                in_head[0] = False
                y_read[0], y_read[1] = bank_read[3], bank_read[4]
            if 0 <= g < NC * len(units):
                up(g)
            if 0 <= g - 1 < NC * len(units):
                cast_h(g - 1)
            if 0 <= g - 2 < NC * len(units):
                low_h(g - 2)
            for b in range(NB):
                if 0 <= s - 4 * b < HEAD_STEPS:
                    head(b, s - 4 * b)
            if s == 1:
                split_w(E, 1, "scalar", "vector")
            if s >= 2 and s % 4 == 2 and s // 4 < E:
                j = s // 4
                if j + 1 < E:
                    load_w(j + 1)
                split_w(j, 0, "scalar", "gpsimd")
            if s >= 2 and s % 4 == 0 and 0 <= s // 4 - 1 < E:
                split_w(s // 4 - 1, 1, "scalar", "gpsimd")
            if s == TOPK_SLOT:
                q = hd[NB - 1]
                head_over = [q["t4"], *w_ready[E - 1, 1], misc["h2l"], misc["h2h"], lg_ready[0]]
                tk_softmax(0)
            if s == TOPK_SLOT + 1:
                tk_softmax(1)
                tk_count(0)
            i = s - TOPK_SLOT - 2
            if 0 <= s - tie0 < 4:
                tk_ties(s - tie0)
            if 0 <= g - NC < NC * len(units):
                down(g - NC)
            if 0 <= i < len(BITS):
                tk_sum(i)
                tk_step(i)
                if i + 1 < len(BITS):
                    tk_count(i + 1)
            if s > tie0 + 3 and gate_next in stash_put:
                gate(gate_next)
                gate_next += 1
            if g >= 2 * NC - 1 and (g + 1) % NC == 0:
                u = (g - NC) // NC
                if u < NB:
                    finish_shared(u)
                elif u < NB + NSTASH:
                    stash(u)
                elif u < len(units):
                    assert gate_next == u, (gate_next, u)
                    gate(u)
                    gate_next += 1
            done = (gate_next - NB) // E
            if pending and s >= pending[0][0]:
                close_b(pending.pop(0)[1])
            if done > len(fin):
                close_a(done - 1)
                if done == NB:
                    close_b(done - 1)
                else:
                    pending.append((s + 3, done - 1))

        block = ctx.enter_context(nc.Block())

        def emit(eng, lane):
            seen = {}
            for after, fn, m, n in lanes[lane].items:
                for name, value in after:
                    if seen.get(name, 0) < value:
                        eng.wait_ge(marks.sems[name][0], value)
                        seen[name] = value
                ins = fn(eng)
                if m:
                    ins.then_inc(marks.sems[m[0]][0], n)

        @block.sync
        def _(eng):
            emit(eng, "sync")
            for name, value in stored[-2:] + g_written[0]:
                eng.wait_ge(marks.sems[name][0], value)

        @block.scalar
        def _(eng):
            emit(eng, "scalar")

        @block.vector
        def _(eng):
            emit(eng, "vector")

        @block.gpsimd
        def _(eng):
            emit(eng, "gpsimd")

        @block.tensor
        def _(eng):
            emit(eng, "tensor")


_INS = ["L0_attn_x", "L0_ffn_gate_weight", "L0_ffn_W1", "L0_ffn_b1", "L0_ffn_W2", "L0_ffn_b2",
        "L0_ffn_Ws1", "L0_ffn_bs1", "L0_ffn_Ws2", "L0_ffn_bs2", "L0_c", "L0_wmod"]


def kernel(**inputs):
    import numpy as _np
    import concourse.bacc as _bacc
    from concourse import mybir as _mybir
    from concourse.bass_utils import run_bass_kernel_spmd as _run

    nc = _bacc.Bacc("TRN2", target_bir_lowering=False, num_devices=1)
    eye = _np.eye(P, dtype=_np.float32)
    tri = _np.triu(_np.ones((P, P), _np.float32))
    consts = _np.concatenate([eye, tri, _np.ones((P, P), _np.float32)], axis=1)
    inv = (1.0 / _np.arange(1, SEQ + 1, dtype=_np.float64)).astype(_np.float32)[None, :]
    given = [(name, _np.ascontiguousarray(inputs[name])) for name in _INS]
    given[0] = (given[0][0], given[0][1].reshape(S, D))
    given += [("consts", consts), ("inv", inv)]
    arrays, args = {}, []
    for name, a in given:
        arrays[f"in_{name}_dram"] = a
        args.append(nc.dram_tensor(f"in_{name}_dram", a.shape, _mybir.dt.from_np(a.dtype), kind="ExternalInput").ap())
    res = nc.dram_tensor("out_0_dram", (S, D), _mybir.dt.float32, kind="ExternalOutput").ap()
    adaln_moe(nc, *args, res)
    r = _run(nc, [arrays], core_ids=[0])
    return _np.asarray(r.results[0]["out_0_dram"]).reshape(2, SEQ, D)
```

```python
from contextlib import ExitStack

import numpy as np

import concourse.bass as bass
from concourse import mybir

ALU = mybir.AluOpType
ACT = mybir.ActivationFunctionType
F32 = mybir.dt.float32
F32R = mybir.dt.float32r
I32 = mybir.dt.int32
U32 = mybir.dt.uint32
F16 = mybir.dt.float16
AX_X = mybir.AxisListType.X

P = 128
D = 128
F = 512
E = 8
NC = F // P
S = 4096
SEQ = 2048
BLK = 512
NB = S // BLK
NT = BLK // P
TOPK = 2 * S
EPS = 1e-5

HEAD_STEPS = 16
UNIT0 = 44
RING = 6
NU = 2 * NB + E - 1
ROW = D + E + D
NPAD = BLK
CW = 2 * BLK
XR = 4
TOPK_SLOT = 4 * (NB - 1) + HEAD_STEPS


class Lane:

    def __init__(self):
        self.items = []


class Marks:

    def __init__(self, new_sem):
        self.new_sem = new_sem
        self.sems = {}

    def raise_(self, name, n):
        if name not in self.sems:
            self.sems[name] = [self.new_sem("s_" + name), 0]
        s = self.sems[name]
        s[1] += n
        return name, s[1]


def adaln_moe(nc, x, gw, w1, b1, w2, b2, ws1, bs1, ws2, bs2, c_in, wmod, consts, ucon, icon, inv, out):
    rows_dram = nc.dram_tensor("rows_scratch", [S + NPAD, ROW], F32, kind="Internal").ap()

    with ExitStack() as ctx:
        def sb(name, shape, dt=F32):
            return ctx.enter_context(nc.sbuf_tensor(name, shape, dt))

        def ps(name):
            return ctx.enter_context(nc.psum_tensor(name, [P, BLK], F32))

        marks = Marks(lambda n: ctx.enter_context(nc.semaphore(n)))
        lanes = {k: Lane() for k in ("sync", "scalar", "vector", "gpsimd", "tensor")}

        def put(lane, fn, after=(), mark=None, n=1):
            m = marks.raise_(mark, n) if mark else None
            lanes[lane].items.append((tuple(a for a in after if a), fn, m, n))
            return m

        def dma(lane, dst, src, mark, after=()):
            return put(lane, lambda e: e.dma_start(dst, src), after, mark, 16)

        W1h, W1l = sb("W1h", [P, E + 1, F], F32R), sb("W1l", [P, E + 1, F], F32R)
        W2h, W2l = sb("W2h", [P, E + 1, NC, D], F32R), sb("W2l", [P, E + 1, NC, D], F32R)
        H2h, H2l = sb("H2h", [P, S], F32R), sb("H2l", [P, S], F32R)
        ACC = sb("ACC", [P, S])
        HF = sb("HF", [P, 4, BLK])
        Hh, Hl = sb("Hh", [P, RING, BLK], F32R), sb("Hl", [P, RING, BLK], F32R)
        TMP = sb("TMP", [P, 2, BLK])
        OUT = sb("OUT", [P, 2, NT, P])
        HT = sb("HT", [P, 2, NT, P])
        R1 = sb("R1", [P, 8192])
        CST = sb("CST", [P, 3 * P])
        COL = sb("COL", [P, 64])
        SM = sb("SM", [P, 192])
        GWh, GWl = sb("GWh", [P, E], F32R), sb("GWl", [P, E], F32R)
        CNT = sb("CNT", [P, 2])
        TI = sb("TI", [P, 4], I32)

        IDENT, TRI, ONES = CST[:, 0:P], CST[:, P:2 * P], CST[:, 2 * P:3 * P]
        XG = R1[:, 0:XR * NT * ROW].rearrange("p (k t c) -> p k t c", k=XR, t=NT)
        YE = R1[:, 4224:5248].rearrange("p (k s) -> p k s", k=2)
        YO = R1[:, 5248:6272].rearrange("p (k t c) -> p k t c", k=2, t=NT)
        WS = R1[:, 3072:5120].rearrange("p (k s) -> p k s", k=2)
        X = R1[:, 0:1536].rearrange("p (k t c) -> p k t c", k=3, t=NT)
        XN = R1[:, 1536:2560].rearrange("p (k t c) -> p k t c", k=2, t=NT)
        XN2 = R1[:, 2560:3072].rearrange("p (t c) -> p t c", t=NT)
        WMOD = R1[:, 5120:5888]
        ROWS = R1[0:64, 5888:6016]
        LR = R1[0:E, 5120:5632]
        CT = R1[:, 6144:7168].rearrange("p (k s) -> p k s", k=2)
        MT = R1[:, 7168:7680]
        INV = sb("INV", [P, 2, BLK])
        H2F = R1[:, 7680:8192]
        TK = R1[:, 6272:7808].rearrange("p (k s) -> p k s", k=6)
        tk = [TK[:, i, :] for i in range(6)]
        GBC = sb("GBC", [P, 2, D])
        UC = sb("UC", [P, NU + E + NT * NU + NT])
        IC = sb("IC", [P, BLK + 2], F16)
        UIOTA, E8 = UC[:, 0:NU], UC[:, NU:NU + E]
        SIG = UC[:, NU + E:NU + E + NT * NU]
        PADR = UC[:, NU + E + NT * NU:NU + E + NT * NU + NT]
        IOTA, DT = IC[:, 0:BLK], IC[:, BLK:BLK + 2]
        CMP = R1[:, 7808:7808 + NU * E].rearrange("p (u e) -> p u e", u=NU)
        OH = R1[:, 8000:8000 + NU * E].rearrange("p (u e) -> p u e", u=NU)
        EX8 = sb("EX8", [P, 6, E])
        EIDF = sb("EIDF", [P, NU])
        EIDI = sb("EIDI", [P, NU], I32)
        UTI = sb("UTI", [P, 2, E], I32)
        IDXB = sb("IDXB", [P, NU, NT], U32)
        STC = sb("STC", [P, 2])
        DQ = sb("DQ", [P, 2, P], F16)
        HM = INV[:, :, :].rearrange("p k s -> p (k s)").bitcast(F16).rearrange("p (k c s) -> p k c s", k=2, c=2)
        CNB = sb("CNB", [P, 4, NT])
        GJ = sb("GJ", [P, P])
        CB1, CB2 = sb("CB1", [P, 2, NC]), sb("CB2", [P, 3, 1])
        GTM, GT4 = sb("GTM", [P, NT, E]), sb("GT4", [P, 2, NT])
        SCT = R1[:, 5888:6144]

        UB = [ps("U0"), ps("U1")]
        YB = [ps("Y0"), ps("Y1")]
        RB = [ps("R0"), ps("R1b"), ps("R2")]
        LG = ps("LG")

        SIL = SM[:, 0:2]
        MOD = SM[:, 2:14]
        MODv = MOD.rearrange("p (h k) -> p h k", h=2)
        SGN = SM[:, 14:18].rearrange("p (h k) -> p h k", h=2)
        MX = SM[:, 18:22].rearrange("p (h k) -> p h k", h=2)
        GG = SM[:, 22:26].rearrange("p (h k) -> p h k", h=2)
        OP = SM[:, 26:30].rearrange("p (h k) -> p h k", h=2)
        CA = SM[:, 30:32]
        CB = SM[:, 32:34]
        GBS = SM[:, 34:36]
        NHALF = SM[:, 36:40]
        KR = SM[:, 40:41]
        ST = SM[:, 64:112].rearrange("p (k t s) -> p k t s", k=2, t=NT)
        MV = SM[:, 112:128].rearrange("p (k t s) -> p k t s", k=2, t=NT)
        VE = SM[:, 128:136].rearrange("p (k t) -> p k t", k=2)
        NM = SM[:, 184:192].rearrange("p (k t) -> p k t", k=2)
        RS = SM[:, 136:152].rearrange("p (k j t) -> p k j t", k=2, j=2)

        ld_cst = dma("sync", CST[:, :], consts, "ld_cst")
        b1r = b1.rearrange("e (c p) -> (e c) p", p=P)
        dma("sync", UC[:, :], ucon, "ld_uc")
        ld_uc = dma("sync", IC[:, :], icon, "ld_uc")
        ld_rows = None
        for dst, src in ((ROWS[0:32, :], b1r), (ROWS[32:36, :], bs1.rearrange("(c p) -> c p", p=P)),
                         (ROWS[36:44, :], b2), (ROWS[44:45, :], bs2.rearrange("(a p) -> a p", a=1)),
                         (ROWS[45:47, :], c_in), (ROWS[47:55, :], gw)):
            ld_rows = dma("scalar", dst, src, "ld_rows")

        x_used = {}

        def load_x(b):
            src = x[b * BLK:(b + 1) * BLK, :].rearrange("(t p) c -> p t c", p=P)
            return dma("sync", X[:, b % 3, :, :], src, f"ld_x{b % 3}", [x_used.get(b - 3)])

        ld_x = {0: load_x(0)}
        ld_wmod = dma("scalar", WMOD, wmod, "ld_wmod")
        ld_x[1] = load_x(1)

        w_used = {}
        ld_w = {}

        def load_w(j):
            k = WORDER.index(j) % 2
            s1 = ws1 if j == E else w1[j]
            s2 = (ws2 if j == E else w2[j]).rearrange("(c p) d -> p c d", p=P)
            free = w_used.get(k, ())
            dma("sync", WS[:, k, 0:F], s1, f"ld_w{k}", free)
            ld_w[j] = dma("sync", WS[:, k, F:2 * F].rearrange("p (c d) -> p c d", c=NC), s2, f"ld_w{k}")

        WORDER = [E] + list(range(E))
        inv_used = {}
        ld_inv = {}

        def load_inv(b):
            q = b % 4
            src = inv[0, q * BLK:(q + 1) * BLK].partition_broadcast(P)
            ld_inv[b] = dma("sync", INV[:, b % 2, :], src, f"ld_inv{b % 2}", [inv_used.get(b - 2)])

        load_w(E)
        load_inv(0)
        load_inv(1)
        ld_x[2] = load_x(2)
        load_w(0)

        nhalf = put("gpsimd", lambda e: e.memset(NHALF, -0.5), mark="nhalf")

        HB = RB + YB
        free_banks = [(k, None) for k in (range(5) if UNIT0 >= 4 * NB else range(3))]

        def give_bank(k, mark):
            free_banks.append((k, mark))

        def take_bank():
            k, mark = free_banks.pop(0)
            return k, HB[k], mark

        kb, bank, free = take_bank()
        m = put("tensor", lambda e, bank=bank: e.transpose(bank[:, 0:55], ROWS[0:55, :], IDENT[0:55, 0:55]),
                [ld_cst, ld_rows], "pe_cols")
        cols = put("vector", lambda e, bank=bank: e.tensor_copy(COL[:, 0:55], bank[:, 0:55]), [m], "v_cols")
        give_bank(kb, cols)
        B1, B2, GWC = COL[:, 0:36], COL[:, 36:45], COL[:, 47:55]
        sil = put("scalar", lambda e: e.activation(SIL, COL[:, 45:47], ACT.Silu), [cols], "a_sil")
        gwh = put("vector", lambda e: e.tensor_copy(GWh[:, :], GWC), [cols], "v_gw")
        gwl = put("vector", lambda e: e.tensor_tensor(GWl[:, :], GWC, GWh[:, :].bitcast(F32), ALU.subtract),
                  [gwh], "v_gw")
        kb, bank, free = take_bank()
        for j in range(6):
            m = put("tensor", lambda e, j=j, bank=bank: e.matmul(
                bank[:, 2 * j:2 * j + 2], WMOD[:, j * P:(j + 1) * P], SIL, start=True, stop=True),
                [sil, ld_wmod], "pe_mod")
        mod = put("vector", lambda e, bank=bank: e.tensor_copy(MOD, bank[:, 0:12]), [m], "v_mod")
        give_bank(kb, mod)
        sgn = put("vector", lambda e: e.tensor_scalar(SGN, MODv[:, :, 4:6], 0.0, 2.0, ALU.is_ge, ALU.mult),
                  [mod], "v_mod")
        pm = put("vector", lambda e: e.tensor_scalar(SGN, SGN, 1.0, None, ALU.subtract), [sgn], "v_mod")
        mxa = put("vector", lambda e: e.tensor_tensor(MX, SGN, MODv[:, :, 4:6], ALU.mult), [pm], "v_mod")
        onep = put("vector", lambda e: e.tensor_scalar(OP, MODv[:, :, 2:4], 1.0, None, ALU.add), [mod], "v_mod")
        gg = put("vector", lambda e: e.scalar_tensor_tensor(GG, MX, 0.25, SGN, ALU.max, ALU.mult), [mxa], "v_mod")
        ca = put("vector", lambda e: e.tensor_tensor(CA, GG[:, 0, :], OP[:, 0, :], ALU.mult), [gg, onep], "v_mod")
        cbm = put("vector", lambda e: e.tensor_tensor(CB, GG[:, 0, :], MODv[:, 0, 0:2], ALU.mult), [gg], "v_mod")
        modv = put("vector", lambda e: e.tensor_scalar(GBS, GG[:, 1, :], B2[:, 8:9], None, ALU.mult),
                   [gg], "v_mod")
        gbd = []
        for n in range(2):
            gbd.append(put("vector", lambda e, n=n: e.tensor_scalar(TMP[:, 0, n * P:(n + 1) * P], IDENT, GG[:, 1, n:n + 1],
                                                                  None, ALU.mult), [gg, ld_cst], "v_gbd"))
        kb, bank, free = take_bank()
        m = put("tensor", lambda e, bank=bank: e.matmul(bank[:, 0:2 * P], ONES, TMP[:, 0, 0:2 * P], start=True, stop=True),
                [gbd[1], free], "pe_gbc")
        gbc = put("vector", lambda e, bank=bank: e.tensor_copy(GBC[:, :, :].rearrange("p n c -> p (n c)"), bank[:, 0:2 * P]),
                  [m], "v_gbc")
        give_bank(kb, gbc)
        zero = put("vector", lambda e: e.memset(OUT[:, 0:2, :, :], 0.0), mark="v_zero")
        half = S // 2
        gb_rows = []
        for n in range(2):
            gb_rows.append(dma("sync", rows_dram[n * half:(n + 1) * half, D + E:ROW].rearrange("(t p) c -> p t c", p=P),
                GBC[:, n, :].unsqueeze(1).to_broadcast([P, half // P, D]), f"st_gb{n}", [gbc]))
        zrow = [dma("sync", out[S:S + NPAD, :].rearrange("(t p) c -> p t c", p=P), OUT[:, 0, :, :], "st_z0", [zero])]
        flat = OUT[:, :, :, :].rearrange("p k t c -> p (k t c)")
        for t in range(NT):
            zrow.append(dma("sync", rows_dram[S + t * P:S + (t + 1) * P, :], flat[:, 0:ROW], f"st_z{1 + t}", [zero]))
        C1, SB2, GBV = OP[:, 1, :], MODv[:, 1, 0:2], GG[:, 1, :]

        w_ready = {}

        def split_w(j, part, act, low):
            k = WORDER.index(j) % 2
            src = WS[:, k, part * F:(part + 1) * F]
            hi = (W1h[:, j, :] if part == 0 else W2h[:, j, :, :].rearrange("p c d -> p (c d)"))
            lo = (W1l[:, j, :] if part == 0 else W2l[:, j, :, :].rearrange("p c d -> p (c d)"))
            if act == "scalar":
                h = put(act, lambda e: e.activation(hi, src, ACT.Copy), [ld_w[j]], "a_w")
            else:
                h = put(act, lambda e: e.tensor_copy(hi, src), [ld_w[j]], "v_w")
            low_m = put(low, lambda e: e.tensor_tensor(lo, src, hi.bitcast(F32), ALU.subtract), [h],
                        {"vector": "v_wl", "gpsimd": "g_wl"}[low])
            w_ready[j, part] = (h, low_m)
            w_used[k] = w_used.get(k, ()) if part else ()
            w_used[k] = w_used[k] + (h, low_m)

        hd = {}
        ct_last = {}
        st_used = {}
        h2_ready = {}
        acc_ready = {}
        lg_ready = [None]
        xn_used = {}
        misc = {}
        ht_used = {}

        def stats(b, src, ready, tag):
            k = {"1": 0, "2": 1}[tag]
            m = None
            for t in range(NT):
                m = put("vector", lambda e, t=t: e.bn_stats(ST[:, k, t, :], src[:, t, :]),
                        [ready, st_used.get(("st", k))] if t == 0 else (), "v_st")
            for t in range(NT):
                a = put("vector", lambda e, t=t: e.bn_aggr(MV[:, k, t, :], ST[:, k, t, :]),
                        [m, st_used.get(("mv", k))] if t == 0 else (), "v_st")
            st_used["st", k] = a
            v = put("gpsimd", lambda e: e.tensor_scalar(VE[:, k, :], MV[:, k, :, 1], 1.0, EPS, ALU.mult, ALU.add),
                    [a], "g_rs")
            if tag == "2":
                g = put("gpsimd", lambda e: e.tensor_scalar(NM[:, k, :], MV[:, k, :, 0], -1.0, 0.0, ALU.mult, ALU.add),
                        [a], "g_rs")
            n = put("gpsimd", lambda e: e.tensor_tensor(RS[:, k, 0, :], VE[:, k, :], NHALF, ALU.pow),
                    [v, nhalf, st_used.get(("rs", k))], "g_rs")
            if tag == "2":
                n = put("gpsimd", lambda e: e.tensor_tensor(RS[:, k, 1, :], NM[:, k, :], RS[:, k, 0, :], ALU.mult),
                        [n, g], "g_rs")
            st_used["mv", k] = n
            return n

        def transposes(dst, src, after, mark):
            for t in range(NT):
                m = put("tensor", lambda e, t=t: e.transpose(dst(t), src(t), IDENT), after if t == 0 else (),
                        mark if t == NT - 1 else None)
            return m

        def head(b, s):
            n = b // 4
            q = hd.setdefault(b, {})
            xs = X[:, b % 3, :, :]
            if s == 0:
                q["nm"] = stats(b, xs, ld_x[b], "1")
            elif s == 2:
                for t in range(NT):
                    q["xn"] = put("vector", lambda e, t=t: e.tensor_scalar(
                        XN[:, b % 2, t, :], xs[:, t, :], MV[:, 0, t, 0:1], RS[:, 0, 0, t:t + 1],
                        ALU.subtract, ALU.mult), [q["nm"], xn_used.get(b - 2)], "v_xn")
                st_used["rs", 0] = st_used["mv", 0] = q["xn"]
            elif s == 3:
                k1, T1, f1 = take_bank()
                q["t1"] = transposes(lambda t: T1[:, t * P:(t + 1) * P], lambda t: XN[:, b % 2, t, :],
                                     [q["xn"], f1], "pe_t1")
                k2, T2, f2 = take_bank()
                q["t2"] = transposes(lambda t: T2[:, t * P:(t + 1) * P], lambda t: xs[:, t, :], [f2], "pe_t2")
                xn_used[b] = q["t1"]
                x_used[b] = q["t2"]
                q["T1"], q["T2"] = (k1, T1), (k2, T2)
                if b + 3 < NB:
                    ld_x[b + 3] = load_x(b + 3)
            elif s == 4:
                k1, T1 = q["T1"]
                k2, T2 = q["T2"]
                first = b % 4 == 0
                init = 0.0 if first else CT[:, (b - 1) % 2, BLK - 1:BLK]
                c = put("vector", lambda e: e.tensor_tensor_scan(
                    CT[:, b % 2, :], ONES[:, 0:1].to_broadcast([P, BLK]), T1[:, :], init, ALU.mult, ALU.add),
                    [q["t1"], ct_last.get(b - 1), ld_cst], "v_ct")
                ct_last[b] = c
                give_bank(k1, c)
                mm = put("vector", lambda e: e.scalar_tensor_tensor(
                    MT, CT[:, b % 2, :], CA[:, n:n + 1], INV[:, b % 2, :], ALU.mult, ALU.mult),
                    [c, ld_inv[b], modv, misc.get("mt")], "v_mt")
                inv_used[b] = mm
                if b + 2 < NB:
                    load_inv(b + 2)
                q["x2"] = put("vector", lambda e: e.scalar_tensor_tensor(
                    ACC[:, b * BLK:(b + 1) * BLK], T2[:, :], CB[:, n:n + 1], MT, ALU.add, ALU.add),
                    [mm, q["t2"]], "v_x2")
                misc["mt"] = q["x2"]
                give_bank(k2, q["x2"])
            elif s == 5:
                k3, T3, f3 = take_bank()
                q["t3"] = transposes(lambda t: T3[:, t * P:(t + 1) * P],
                                     lambda t: ACC[:, b * BLK + t * P:b * BLK + (t + 1) * P],
                                     [q["x2"], f3], "pe_t3")
                q["T3"] = (k3, T3)
                acc_ready[b] = q["t3"]
            elif s == 6:
                k3, T3 = q["T3"]
                q["nm2"] = stats(b, T3[:, :].rearrange("p (t c) -> p t c", t=NT), q["t3"], "2")
            elif s == 8:
                k3, T3 = q["T3"]
                for t in range(NT):
                    m = put("scalar", lambda e, t=t: e.activation(
                        XN2[:, t, :], T3[:, t * P:(t + 1) * P], ACT.Identity,
                        bias=RS[:, 1, 1, t:t + 1], scale=RS[:, 1, 0, t:t + 1]),
                        [q["nm2"], misc.get("xn2")], "a_xn2")
                q["xn2"] = m
                st_used["rs", 1] = m
                give_bank(k3, m)
            elif s == 9:
                k4, T4, f4 = take_bank()
                q["t4"] = transposes(lambda t: T4[:, t * P:(t + 1) * P], lambda t: XN2[:, t, :],
                                     [q["xn2"], f4], "pe_t4")
                misc["xn2"] = q["t4"]
                q["T4"] = (k4, T4)
            elif s == 10:
                k4, T4 = q["T4"]
                f = put("scalar", lambda e: e.activation(H2F, T4[:, :], ACT.Identity, bias=SB2[:, n:n + 1],
                                                         scale=C1[:, n:n + 1]),
                        [q["t4"], misc.get("h2l"), misc.get("h2h"), misc.get("h2t")], "a_h2f")
                give_bank(k4, f)
                h = put("scalar", lambda e: e.activation(H2h[:, b * BLK:(b + 1) * BLK], H2F, ACT.Copy), [f], "a_h2")
                q["h2h"] = h
            elif s == 11:
                h = q["h2h"]
                lo = put("vector", lambda e: e.tensor_tensor(
                    H2l[:, b * BLK:(b + 1) * BLK], H2F, H2h[:, b * BLK:(b + 1) * BLK].bitcast(F32), ALU.subtract),
                    [h], "v_h2l")
                misc["h2l"], misc["h2h"] = lo, h
                h2_ready[b] = (h, lo)
            elif s == 12:
                k6, T6, f6 = take_bank()
                q["t6"] = transposes(lambda t: T6[:, t * P:(t + 1) * P], lambda t: H2F[:, t * P:(t + 1) * P],
                                     [q["h2h"], f6], "pe_t6")
                q["T6"] = (k6, T6)
                misc["h2t"] = q["t6"]
            elif s == 13:
                k6, T6 = q["T6"]
                m = put("scalar", lambda e: e.activation(HT[:, b % 2, :, :].rearrange("p t c -> p (t c)"), T6[:, :],
                                                         ACT.Copy), [q["t6"], ht_used.get(b - 2)], "a_ht")
                give_bank(k6, m)
                ht_used[b] = dma("sync", rows_dram[b * BLK:(b + 1) * BLK, 0:D].rearrange("(t p) c -> p t c", p=P),
                                 HT[:, b % 2, :, :], f"st_ht{b % 2}", [m])
            elif s == 14:
                k5, T5, f5 = take_bank()
                hs, ls = H2h[:, b * BLK:(b + 1) * BLK], H2l[:, b * BLK:(b + 1) * BLK]
                for i, (a, r) in enumerate(((GWh, hs), (GWh, ls), (GWl, hs))):
                    m = put("tensor", lambda e, a=a, r=r, i=i: e.matmul(
                        T5[0:E, :], a[:, :], r, start=i == 0, stop=i == 2),
                        [*h2_ready[b], gwl, f5] if i == 0 else (), "pe_lr" if i == 2 else None)
                q["lr"], q["T5"] = m, (k5, T5)
            elif s == 15:
                k5, T5 = q["T5"]
                m = put("scalar", lambda e: e.activation(LR, T5[0:E, :], ACT.Copy),
                        [q["lr"], misc.get("lrt"), mod], "a_lr")
                give_bank(k5, m)
                for t in range(NT):
                    j = (b * NT + t) * E
                    mt = put("tensor", lambda e, t=t, j=j: e.transpose(
                        LG[:, j:j + E], LR[:, t * P:(t + 1) * P], IDENT[0:E, 0:E]), [m],
                        "pe_lg" if t == NT - 1 else None)
                misc["lrt"] = mt
                lg_ready[0] = mt

        units = [(E, b) for b in range(NB)] + [(None, v) for v in range(NU)]
        gelu, cast, low, h_used = {}, {}, {}, {}
        up_done = {}
        u_read = [None, None]
        y_read = [None, None]
        y_done = {}
        xt_ready = {}
        cw1_ready, cw2_ready = {}, {}
        CWS = [H2h[:, CW:CW + 4 * BLK], H2l[:, CW:CW + 4 * BLK]]

        def up(g):
            u = g // NC
            j, b = units[u]
            c = g % NC
            bank = UB[g % 2]
            if u < NB:
                wh, wl = W1h[:, j, c * P:(c + 1) * P], W1l[:, j, c * P:(c + 1) * P]
                hs, ls = H2h[:, b * BLK:(b + 1) * BLK], H2l[:, b * BLK:(b + 1) * BLK]
                bias = B1[:, j * NC + c:j * NC + c + 1]
                need = [*h2_ready[b], *w_ready[j, 0]]
            else:
                k = b % 2
                wh, wl = CWS[k][:, c * P:(c + 1) * P], CWS[k][:, BLK + c * P:BLK + (c + 1) * P]
                hs, ls = H2h[:, k * BLK:(k + 1) * BLK], H2l[:, k * BLK:(k + 1) * BLK]
                bias = CB1[:, k, c:c + 1]
                need = [*xt_ready[b], *cw1_ready[b]]
            for i, (a, r) in enumerate(((wh, hs), (wh, ls), (wl, hs))):
                m = put("tensor", lambda e, a=a, r=r, i=i: e.matmul(bank[:, :], a, r, start=i == 0, stop=i == 2),
                        [*need, u_read[g % 2]] if i == 0 else (), "pe_up" if i == 2 else None)
            up_done[g] = m
            gelu[g] = put("scalar", lambda e: e.activation(HF[:, g % 4, :], bank[:, :], ACT.Gelu_apprx_tanh, bias=bias),
                          [m, low.get(g - 4), cast.get(g - 4), cols], "a_gelu")
            u_read[g % 2] = gelu[g]

        def cast_h(g):
            hi, src = Hh[:, g % RING, :], HF[:, g % 4, :]
            if g % NC == 1:
                cast[g] = put("vector", lambda e: e.tensor_copy(hi, src), [gelu[g], h_used.get(g - RING)], "v_cast")
            else:
                cast[g] = put("scalar", lambda e: e.activation(hi, src, ACT.Copy),
                              [gelu[g], h_used.get(g - RING)], "a_cast")

        def low_h(g):
            hi, lo, src = Hh[:, g % RING, :], Hl[:, g % RING, :], HF[:, g % 4, :]
            low[g] = put("vector", lambda e: e.tensor_tensor(lo, src, hi.bitcast(F32), ALU.subtract),
                         [cast[g], h_used.get(g - RING)], "v_low")

        def down(g):
            u = g // NC
            j, b = units[u]
            c = g % NC
            bank = YB[u % 2]
            if u < NB:
                wh, wl = W2h[:, j, c, :], W2l[:, j, c, :]
                need = w_ready[j, 1]
            else:
                w = CWS[b % 2]
                wh, wl = w[:, 2 * BLK + c * P:2 * BLK + (c + 1) * P], w[:, 3 * BLK + c * P:3 * BLK + (c + 1) * P]
                need = cw2_ready[b]
            hi, lo = Hh[:, g % RING, :], Hl[:, g % RING, :]
            for i, (a, r) in enumerate(((wh, hi), (wh, lo), (wl, hi))):
                m = put("tensor", lambda e, a=a, r=r, i=i: e.matmul(
                    bank[:, :], a, r, start=(c == 0 and i == 0), stop=(c == NC - 1 and i == 2)),
                    [cast[g], low[g], *need, y_read[u % 2] if c == 0 else None] if i == 0 else (),
                    "pe_dn" if i == 2 else None)
            h_used[g] = m
            if c == NC - 1:
                y_done[u] = m

        tmp_used = [None, None]
        tmp_next = [0]
        out_free = [zrow[-1], zrow[-1]]
        shared_done = {}
        stored = []

        def finish_shared(u):
            b = units[u][1]
            n = b // 4
            bank = YB[u % 2]
            k = tmp_next[0] % 2
            tmp_next[0] += 1
            a = put("scalar", lambda e: e.activation(TMP[:, k, :], bank[:, :], ACT.Identity,
                                                     bias=GBS[:, n:n + 1], scale=GBV[:, n:n + 1]),
                    [y_done[u], tmp_used[k], modv, gbc], "a_sh")
            y_read[u % 2] = a
            acc = ACC[:, b * BLK:(b + 1) * BLK]
            tmp_used[k] = shared_done[b] = put(
                "gpsimd", lambda e: e.tensor_tensor(acc, acc, TMP[:, k, :], ALU.add), [a, acc_ready[b]], "g_sh")

        def close(b):
            k, bank, free = take_bank()
            m = transposes(lambda t: bank[:, t * P:(t + 1) * P],
                           lambda t: ACC[:, b * BLK + t * P:b * BLK + (t + 1) * P], [shared_done[b], free], "pe_out")
            o = put("scalar", lambda e: e.activation(OUT[:, b % 2, :, :].rearrange("p t c -> p (t c)"), bank[:, :],
                                                     ACT.Copy), [m, out_free[b % 2]], "a_out")
            give_bank(k, o)
            dst = out[b * BLK:(b + 1) * BLK, :].rearrange("(t p) c -> p t c", p=P)
            out_free[b % 2] = dma("sync", dst, OUT[:, b % 2, :, :], f"st_out{b % 2}", [o])
            stored.append(out_free[b % 2])

        idx_ready, gathered, xt_done, yo_done, xl_of = {}, {}, {}, {}, {}
        ye_done, yt_done, scattered = {}, {}, {}
        hm_ready, g_done, g_read = {}, {}, {}
        reg = {}

        def idx_mask(v):
            for ch in range(2):
                m = put("vector", lambda e, ch=ch: e.tensor_scalar(
                    HM[:, v % 2, ch, :], IOTA, STC[:, ch:ch + 1], float(-BLK * v), ALU.subtract, ALU.is_ge),
                    [tkm["stc"], g_done.get(v - 2), ld_uc], "v_hm")
            hm_ready[v] = m

        def idx_mm(v):
            bank = RB[2]
            for s in range(NT):
                for ch in range(2):
                    lhs = HM[:, v % 2, ch, s * P:(s + 1) * P]
                    put("tensor", lambda e, s=s, ch=ch, lhs=lhs: e.matmul(
                        bank[:, s * P:(s + 1) * P], lhs, DQ[:, ch, :], start=ch == 0, stop=ch == 1),
                        [hm_ready[v], tkm["dq"], g_read.get(v - 1), *tkm["banks"]] if s == 0 and ch == 0 else ())
                for ch in range(2):
                    lhs = HM[:, v % 2, ch, s * P:(s + 1) * P]
                    m = put("tensor", lambda e, s=s, ch=ch, lhs=lhs: e.matmul(
                        LG[:, s:s + 1], lhs, DT[:, ch:ch + 1], start=ch == 0, stop=ch == 1),
                        (), "pe_idx" if s == NT - 1 and ch == 1 else None)
            g_done[v] = m

        def idx_count(v):
            bank = RB[2]
            c0, c1, c2, c3 = (CNB[:, i, :] for i in range(4))
            m = idx_ready.get(v - 1)
            for s in range(NT):
                i = NT * v + s
                m = put("vector", lambda e, s=s, i=i: e.tensor_scalar(
                    GJ[:, :], bank[:, s * P:(s + 1) * P], SIG[:, i:i + 1], None, ALU.is_le, ALU.add,
                    accum_out=c0[:, s:s + 1]), [g_done[v], m], "v_idx")
            a = put("vector", lambda e: e.tensor_tensor(c1, c0, LG[:, 0:NT], ALU.add), [m], "v_idx")
            g_read[v] = a
            b = put("vector", lambda e: e.tensor_tensor(c2, PADR, c1, ALU.subtract), [a], "v_idx")
            c = put("vector", lambda e: e.scalar_tensor_tensor(c3, c0, float(P), c2, ALU.is_ge, ALU.mult), [b], "v_idx")
            idx_ready[v] = put("vector", lambda e: e.tensor_tensor(IDXB[:, v, :], c1, c3, ALU.add), [c], "v_idx")

        def gather(v):
            for s in range(NT):
                m = put("gpsimd", lambda e, s=s: e.indirect_dma_start(
                    XG[:, v % XR, s, :], None, rows_dram, bass.IndirectOffsetOnAxis(ap=IDXB[:, v, s:s + 1], axis=0)),
                    [idx_ready[v], yo_done.get(v - XR), xt_done.get(v - XR), *tkm["rows"]], f"ld_xg{v % XR}", 16)
            gathered[v] = m

        def xt(v):
            bank = RB[0]
            xt_done[v] = transposes(lambda t: bank[:, t * P:(t + 1) * P], lambda t: XG[:, v % XR, t, 0:D],
                                    [gathered[v], *xl_of.get(v - 1, ()), *tkm["banks"]], "pe_xt")

        def split_x(v):
            bank = RB[0]
            k = v % 2
            hi, lo = H2h[:, k * BLK:(k + 1) * BLK], H2l[:, k * BLK:(k + 1) * BLK]
            free = up_done[NC * (NB + v - 2) + NC - 1] if v >= 2 else up_done[NC * NB - 1]
            h = put("scalar", lambda e: e.activation(hi, bank[:, :], ACT.Copy), [xt_done[v], free], "a_xh")
            lo_m = put("vector", lambda e: e.tensor_tensor(lo, bank[:, :], hi.bitcast(F32), ALU.subtract), [h, free],
                       "v_xl")
            xl_of[v] = (h, lo_m)
            xt_ready[v] = (h, lo_m)

        def weights(v, part, lane, half):
            dst = CWS[v % 2][:, (2 * part + half) * BLK:(2 * part + half + 1) * BLK]
            src = ((W1h, W1l), (W2h, W2l))[part][half]
            if part == 0:
                src = src[:, :, :]
            else:
                src = src[:, :, :, :].rearrange("p e c d -> p e (c d)")
            src = src.bitcast(F32)
            free = up_done[NC * NB - 1]
            if v >= 2:
                free = up_done[NC * (NB + v - 2) + NC - 1] if part == 0 else h_used[NC * (NB + v - 2) + NC - 1]
            need = [tkm["eid"], free, *w_ready[E - 1, part], *(h2_over if v < 2 else ())]

            def fn(e, lane=lane):
                if (lane, v) not in reg:
                    reg[lane, v] = e.value_load(EIDI[0:1, v:v + 1], min_val=0, max_val=E - 1)
                a = src[:, bass.ds(reg[lane, v], 1), :].rearrange("p a n -> p (a n)")
                return e.activation(dst, a, ACT.Copy) if lane == "scalar" else e.tensor_copy(dst, a)

            return put(lane, fn, need, {"scalar": "a_cw", "vector": "v_cw"}[lane])

        def bias_cols(v):
            k = v % 2

            def fn1(e):
                if ("vector", v) not in reg:
                    reg["vector", v] = e.value_load(EIDI[0:1, v:v + 1], min_val=0, max_val=E - 1)
                a = B1[:, 0:E * NC].rearrange("p (e c) -> p e c", e=E)[:, bass.ds(reg["vector", v], 1), :]
                return e.tensor_copy(CB1[:, k, :], a.rearrange("p a n -> p (a n)"))

            def fn2(e):
                return e.tensor_copy(CB2[:, v % 3, :], B2[:, bass.ds(reg["vector", v], 1)])

            g = NC * (NB + v - 2) + NC - 1
            m = put("vector", fn1, [tkm["eid"], gelu.get(g) if v >= 2 else None], "v_cb")
            return m, put("vector", fn2, [ye_done.get(v - 3)], "v_cb")

        def weights_a(v):
            cb = bias_cols(v)
            cw1_ready[v] = [weights(v, 0, "scalar", 0), weights(v, 0, "vector", 1), *cb]

        def weights_b(v):
            cw2_ready[v] = [weights(v, 1, "scalar", 0), weights(v, 1, "scalar", 1)]

        def ye(v):
            u = NB + v
            bank = YB[u % 2]
            ye_done[v] = put("scalar", lambda e: e.activation(YE[:, v % 2, :], bank[:, :], ACT.Identity,
                                                             bias=CB2[:, v % 3, :]),
                             [y_done[u], yt_done.get(v - 2), cw1_ready[v][3], *head_over], "a_ye")
            y_read[u % 2] = ye_done[v]

        def yt(v):
            bank = RB[1]
            yt_done[v] = transposes(lambda t: bank[:, t * P:(t + 1) * P], lambda t: YE[:, v % 2, t * P:(t + 1) * P],
                                    [ye_done[v], yo_done.get(v - 1), *tkm["banks"]], "pe_yt")

        def yo(v):
            bank = RB[1]
            k, r = v % 2, v % XR
            a = put("vector", lambda e: e.tensor_tensor(
                GTM[:, :, :], XG[:, r, :, D:D + E], OH[:, v, :].unsqueeze(1).to_broadcast([P, NT, E]), ALU.mult),
                [gathered[v], tkm["oh"], gt_last[0]], "v_gt")
            b = put("vector", lambda e: e.tensor_reduce(GT4[:, k, :], GTM[:, :, :], AX_X, ALU.add),
                    [a, yo_done.get(v - 2)], "v_gt")
            gt_last[0] = b
            for t in range(NT):
                m = put("vector", lambda e, t=t: e.scalar_tensor_tensor(
                    YO[:, k, t, :], bank[:, t * P:(t + 1) * P], GT4[:, k, t:t + 1], XG[:, r, t, D + E:ROW],
                    ALU.mult, ALU.mult), [b, yt_done[v], scattered.get(v - 2)], "v_yo")
            yo_done[v] = m

        gt_last = [None]

        def scatter(v):
            prev = scattered.get(v - 1)
            for s in range(NT):
                m = put("gpsimd", lambda e, s=s: e.indirect_dma_start(
                    out, bass.IndirectOffsetOnAxis(ap=IDXB[:, v, s:s + 1], axis=0), YO[:, v % 2, s, :], None,
                    compute_op=ALU.add, bounds_check=S + NPAD - 1, oob_is_err=True),
                    [yo_done[v], prev, *(stored[-2:] + zrow if v == 0 else ())], f"st_sc{v % 2}", 16)
            scattered[v] = m

        SC, EX, GT, EQ, CUMX, RK = tk
        SEL = EX
        SCv = SC.rearrange("p (e t) -> p e t", e=E)
        tkm = {}
        T_I, C_I, M_I = TI[:, 0:1], TI[:, 1:2], TI[:, 2:3]
        MXR, SMR, RCR = SM[:, 152:184], COL[:, 0:1], None
        RED = sb("RED", [P, 3, NB * NT])
        LGv = LG[:, 0:256].rearrange("p (t e) -> p t e", e=E)
        BITS = list(range(29, -1, -1))

        def tk_softmax(step):
            EXv = EX.rearrange("p (t e) -> p t e", e=E)
            if step == 0:
                a = put("vector", lambda e: e.tensor_reduce(RED[:, 0, :], LGv, AX_X, ALU.max), [lg_ready[0]], "v_tk")
                tkm["sub"] = put("vector", lambda e: e.tensor_tensor(
                    EXv, LGv, RED[:, 0, :].unsqueeze(2).to_broadcast([P, NB * NT, E]), ALU.subtract),
                    [a, *head_over], "v_tk")
                tkm["exp"] = put("scalar", lambda e: e.activation(EX, EX, ACT.Exp), [tkm["sub"]], "a_exp")
            else:
                a = put("vector", lambda e: e.tensor_reduce(RED[:, 1, :], EXv, AX_X, ALU.add), [tkm["exp"]], "v_tk")
                r = put("vector", lambda e: e.reciprocal(RED[:, 2, :], RED[:, 1, :]), [a], "v_tk")
                tkm["sc"] = put("vector", lambda e: e.tensor_tensor(
                    SCv.rearrange("p e t -> p t e"), EXv,
                    RED[:, 2, :].unsqueeze(2).to_broadcast([P, NB * NT, E]), ALU.mult), [r], "v_tk")
                t = put("gpsimd", lambda e: e.tensor_copy(SCT.rearrange("p (t e) -> p t e", e=E),
                                                          SCv.rearrange("p e t -> p t e")), [tkm["sc"]], "g_sct")
                st = dma("sync", rows_dram[0:S, D:D + E].rearrange("(t p) e -> p t e", p=P),
                         SCT.rearrange("p (t e) -> p t e", e=E), "st_sc", [t])
                tkm["rows"] = [st, *(ht_used[b] for b in (NB - 2, NB - 1)), *gb_rows, *zrow]
                z = put("vector", lambda e: e.memset(T_I, 0), mark="v_tk")
                tkm["t"] = z
                tkm["cand"] = put("vector", lambda e: e.memset(C_I, 1 << BITS[0]), mark="v_tk")

        def tk_count(i):
            tkm["cnt"] = put("vector", lambda e: e.tensor_scalar(
                GT, SC, C_I.bitcast(F32), None, ALU.is_ge, ALU.add, accum_out=CNT[:, i % 2:i % 2 + 1]),
                [tkm["sc"], tkm["cand"]], "v_cnt")

        def tk_sum(i):
            tkm["sum"] = put("tensor", lambda e: e.matmul(LG[:, 256 + i % 2:257 + i % 2], ONES,
                                                          CNT[:, i % 2:i % 2 + 1], start=True, stop=True),
                             [tkm["cnt"]], "pe_sum")

        def tk_step(i):
            bit = BITS[i]
            m = put("vector", lambda e: e.tensor_scalar(M_I, LG[:, 256 + i % 2:257 + i % 2], float(TOPK),
                                                        float(1 << bit), ALU.is_ge, ALU.mult),
                    [tkm["sum"], tkm["t"]], "v_tk")
            if bit:
                tkm["cand"] = put("vector", lambda e: e.scalar_tensor_tensor(
                    C_I, M_I, 1 << (bit - 1), T_I, ALU.bitwise_or, ALU.bitwise_or), [m, tkm["cnt"]], "v_cand")
            tkm["t"] = put("vector", lambda e: e.tensor_tensor(T_I, T_I, M_I, ALU.bitwise_or),
                           [m, tkm["t"], tkm["cand"]], "v_tk")

        def tk_ties(s):
            TF = T_I.bitcast(F32)
            if s == 0:
                a = put("vector", lambda e: e.tensor_scalar(GT, SC, TF, None, ALU.is_gt, ALU.add,
                                                            accum_out=CNT[:, 0:1]), [tkm["t"], tkm["cnt"]], "v_tk")
                q = put("vector", lambda e: e.tensor_scalar(EQ, SC, TF, None, ALU.is_equal), [tkm["t"]], "v_tk")
                tkm["masks"] = q
            elif s == 1:
                k, bank, free = take_bank()
                put("tensor", lambda e: e.matmul(LG[:, 260:261], ONES, CNT[:, 0:1], start=True, stop=True),
                    [tkm["masks"]])
                put("tensor", lambda e: e.matmul(bank[:, 0:256], TRI, EQ, start=True, stop=True), [free])
                m = put("tensor", lambda e: e.matmul(bank[:, 256:512], ONES, EQ, start=True, stop=True),
                        mark="pe_tie")
                r = put("vector", lambda e: e.tensor_scalar(KR, LG[:, 260:261], -1.0, float(TOPK), ALU.mult, ALU.add),
                        [m], "v_tk")
                c = put("vector", lambda e: e.tensor_tensor_scan(
                    CUMX, ONES[:, 0:1].to_broadcast([P, 256]), bank[:, 256:512], 0.0, ALU.mult, ALU.add), [m], "v_tk")
                c2 = put("vector", lambda e: e.tensor_tensor(RK, CUMX, bank[:, 256:512], ALU.subtract), [c], "v_tk")
                c3 = put("vector", lambda e: e.tensor_tensor(RK, RK, bank[:, 0:256], ALU.add), [c2], "v_tk")
                give_bank(k, c3)
                tkm["rk"] = c3
            elif s == 2:
                a = put("vector", lambda e: e.scalar_tensor_tensor(SEL, RK, KR, EQ, ALU.is_le, ALU.mult),
                        [tkm["rk"]], "v_tk")
                a = put("vector", lambda e: e.tensor_tensor(SEL, SEL, GT, ALU.add), [a], "v_tk")
                tkm["sel"] = a
            elif s == 3:
                k, bank, free = take_bank()
                put("tensor", lambda e: e.matmul(bank[:, 0:256], ONES, SEL, start=True, stop=True), [tkm["sel"], free])
                m = put("tensor", lambda e: e.matmul(bank[:, 256:512], TRI, SEL, start=True, stop=True), (), "pe_cum")
                TOT, CUM = bank[:, 0:256], bank[:, 256:512]
                NE, UT, UE, OFF = (EX8[:, i, :] for i in range(4))

                def v(fn, after):
                    return put("vector", fn, after, "v_ds")

                n = v(lambda e: e.tensor_reduce(NE, TOT.rearrange("p (e t) -> p e t", e=E), AX_X, ALU.add), [m])
                c = v(lambda e: e.tensor_tensor_scan(CUMX, ONES[:, 0:1].to_broadcast([P, 256]), TOT, 0.0,
                                                     ALU.mult, ALU.add), [n])
                n = v(lambda e: e.tensor_scalar(UTI[:, 0, :], NE, 1.0, float(BLK - 1), ALU.mult, ALU.add), [n])
                x_ = v(lambda e: e.tensor_tensor(RK, CUMX, TOT, ALU.subtract), [c])
                n = v(lambda e: e.tensor_scalar(UTI[:, 1, :], UTI[:, 0, :], 9, None, ALU.logical_shift_right), [n])
                n = v(lambda e: e.tensor_scalar(UT, UTI[:, 1, :], 1.0, None, ALU.max), [n])
                n = v(lambda e: e.tensor_tensor_scan(UE, ONES[:, 0:1].to_broadcast([P, E]), UT, 0.0,
                                                     ALU.mult, ALU.add), [n])
                o = v(lambda e: e.tensor_tensor(OFF, UE, UT, ALU.subtract), [n])
                EXC0 = RK.rearrange("p (e t) -> p e t", e=E)[:, :, 0]
                o = v(lambda e: e.scalar_tensor_tensor(OFF, OFF, float(BLK), EXC0, ALU.mult, ALU.subtract), [o, x_])
                o = v(lambda e: e.tensor_tensor(GT.rearrange("p (e t) -> p e t", e=E),
                                                RK.rearrange("p (e t) -> p e t", e=E),
                                                OFF.unsqueeze(2).to_broadcast([P, E, NB * NT]), ALU.add), [o])
                q = v(lambda e: e.tensor_tensor(EQ, GT, CUM, ALU.add), [o])
                give_bank(k, q)
                q = v(lambda e: e.tensor_tensor(CUMX[:, 1:256], EQ[:, 1:256], EQ[:, 0:255], ALU.subtract), [q])
                q = v(lambda e: e.tensor_copy(CUMX[:, 0:1], EQ[:, 0:1]), [q])
                tkm["dqf"], tkm["start"] = q, o
            elif s == 4:
                k, bank, free = take_bank()
                for h in range(2):
                    put("tensor", lambda e, h=h: e.transpose(bank[:, h * P:(h + 1) * P],
                                                             CUMX[:, h * P:(h + 1) * P], IDENT),
                        [tkm["dqf"], tkm["start"], free])
                for h in range(2):
                    m = put("tensor", lambda e, h=h: e.transpose(bank[:, (2 + h) * P:(3 + h) * P],
                                                                 GT[:, h * P:(h + 1) * P], IDENT), (), "pe_dq")
                tkm["stc"] = put("vector", lambda e: e.tensor_copy(
                    STC[:, :], bank[:, 256:512].rearrange("p (k q) -> p k q", k=2)[:, :, 0]), [m], "v_ds")
                c = put("scalar", lambda e: e.activation(DQ[:, :, :].rearrange("p k q -> p (k q)"), bank[:, 0:256],
                                                         ACT.Copy), [tkm["stc"]], "a_dq")
                tkm["dq"] = c
                give_bank(k, c)
                tkm["banks"] = [mk for _, mk in free_banks]
                idx_mask(0)
                UE = EX8[:, 2, :]
                a = put("vector", lambda e: e.tensor_tensor(
                    CMP[:, :, :], UE.unsqueeze(1).to_broadcast([P, NU, E]),
                    UIOTA.unsqueeze(2).to_broadcast([P, NU, E]), ALU.is_le), [tkm["start"], ld_uc], "v_eid")
                a = put("vector", lambda e: e.tensor_reduce(EIDF[:, :], CMP[:, :, :], AX_X, ALU.add), [a], "v_eid")
                a = put("vector", lambda e: e.tensor_scalar(EIDF[:, :], EIDF[:, :], float(E - 1), None, ALU.min),
                        [a], "v_eid")
                tkm["eid"] = put("vector", lambda e: e.tensor_copy(EIDI[:, :], EIDF[:, :]), [a], "v_eid")
                idx_mm(0)
                idx_count(0)
                gather(0)
                tkm["oh"] = put("vector", lambda e: e.tensor_tensor(
                    OH[:, :, :], EIDF[:, :].unsqueeze(2).to_broadcast([P, NU, E]),
                    E8.unsqueeze(1).to_broadcast([P, NU, E]), ALU.is_equal), [a], "v_eid")
                idx_mask(1)
                idx_mm(1)
                idx_count(1)
                gather(1)
            elif s == 5:
                weights_a(0)
                weights_b(0)
                xt(0)
                split_x(0)

        tie0 = TOPK_SLOT + 3 + len(BITS)
        UNIT1 = tie0 + 6
        NG = NC * len(units)
        GS = {UNIT0 + g: g for g in range(NC * NB)}
        GS.update({UNIT1 + g - NC * NB: g for g in range(NC * NB, NG)})
        head_over = []
        h2_over = []
        split_w(E, 0, "scalar", "vector")
        n_closed = 0
        for s in range(UNIT1 + NC * (NU + 4)):
            if s == UNIT0 and UNIT0 >= 4 * NB:
                for k, mark in [f for f in free_banks if f[0] >= 3]:
                    y_read[k - 3] = mark
                    free_banks.remove((k, mark))
            if s in GS:
                up(GS[s])
            if s - 1 in GS:
                cast_h(GS[s - 1])
            if s - 2 in GS:
                low_h(GS[s - 2])
            for b in range(NB):
                if 0 <= s - 4 * b < HEAD_STEPS:
                    head(b, s - 4 * b)
            if s == 1:
                split_w(E, 1, "scalar", "vector")
            if s % 3 == 2 and s // 3 < 2 * E:
                j, part = s // 3 // 2, s // 3 % 2
                if part == 0 and j + 1 < E:
                    load_w(j + 1)
                split_w(j, part, "scalar", "gpsimd")
            if s == TOPK_SLOT:
                q = hd[NB - 1]
                head_over = [q["t4"], misc["h2l"], misc["h2h"], misc["h2t"], lg_ready[0]]
                h2_over = [lg_ready[0], misc["lrt"], hd[NB - 1]["lr"]]
                tk_softmax(0)
            if s == TOPK_SLOT + 1:
                tk_softmax(1)
                tk_count(0)
            i = s - TOPK_SLOT - 2
            if s - 4 in GS and GS[s - 4] < NC * NB:
                g = GS[s - 4]
                down(g)
                if g % NC == NC - 1:
                    finish_shared(g // NC)
            if s - 6 in GS and GS[s - 6] % NC == NC - 1 and GS[s - 6] < NC * NB:
                close(GS[s - 6] // NC)
            if 0 <= s - tie0 < 6:
                tk_ties(s - tie0)
            if 0 <= i < len(BITS):
                tk_sum(i)
                tk_step(i)
                if i + 1 < len(BITS):
                    tk_count(i + 1)
            v, c = (s - UNIT1) // NC, (s - UNIT1) % NC
            if v >= 0:
                if c == 0:
                    if 0 <= v - 2 < NU:
                        ye(v - 2)
                    if 0 < v < NU:
                        weights_b(v)
                    if v + 2 < NU:
                        idx_mask(v + 2)
                elif c == 1:
                    if 0 <= v - 2 < NU:
                        yt(v - 2)
                    if v + 2 < NU:
                        idx_mm(v + 2)
                    if v + 1 < NU:
                        weights_a(v + 1)
                elif c == 2:
                    if 0 <= v - 2 < NU:
                        yo(v - 2)
                        scatter(v - 2)
                    if v + 1 < NU:
                        xt(v + 1)
                    if v + 2 < NU:
                        idx_count(v + 2)
                        gather(v + 2)
                elif c == 3:
                    if v + 1 < NU:
                        split_x(v + 1)
                if s - 4 in GS and GS[s - 4] >= NC * NB:
                    down(GS[s - 4])

        block = ctx.enter_context(nc.Block())

        def emit(eng, lane):
            seen = {}
            for after, fn, m, n in lanes[lane].items:
                for name, value in after:
                    if seen.get(name, 0) < value:
                        eng.wait_ge(marks.sems[name][0], value)
                        seen[name] = value
                ins = fn(eng)
                if m:
                    ins.then_inc(marks.sems[m[0]][0], n)

        @block.sync
        def _(eng):
            emit(eng, "sync")

        @block.scalar
        def _(eng):
            emit(eng, "scalar")

        @block.vector
        def _(eng):
            emit(eng, "vector")

        @block.gpsimd
        def _(eng):
            emit(eng, "gpsimd")
            for name, value in (scattered[NU - 2], scattered[NU - 1]):
                eng.wait_ge(marks.sems[name][0], value)

        @block.tensor
        def _(eng):
            emit(eng, "tensor")


_INS = ["L0_attn_x", "L0_ffn_gate_weight", "L0_ffn_W1", "L0_ffn_b1", "L0_ffn_W2", "L0_ffn_b2",
        "L0_ffn_Ws1", "L0_ffn_bs1", "L0_ffn_Ws2", "L0_ffn_bs2", "L0_c", "L0_wmod"]


def kernel(**inputs):
    import numpy as _np
    import concourse.bacc as _bacc
    from concourse import mybir as _mybir
    from concourse.bass_utils import run_bass_kernel_spmd as _run

    nc = _bacc.Bacc("TRN2", target_bir_lowering=False, num_devices=1)
    eye = _np.eye(P, dtype=_np.float32)
    tri = _np.triu(_np.ones((P, P), _np.float32))
    consts = _np.concatenate([eye, tri, _np.ones((P, P), _np.float32)], axis=1)
    inv = (1.0 / _np.arange(1, SEQ + 1, dtype=_np.float64)).astype(_np.float32)[None, :]
    given = [(name, _np.ascontiguousarray(inputs[name])) for name in _INS]
    given[0] = (given[0][0], given[0][1].reshape(S, D))
    nu = NU
    ucon = _np.zeros((P, nu + E + NT * nu + NT), _np.float32)
    ucon[:, 0:nu] = _np.arange(nu)
    ucon[:, nu:nu + E] = _np.arange(E)
    part = _np.arange(P)[:, None]
    ucon[:, nu + E:nu + E + NT * nu] = _np.arange(NT * nu)[None, :] * P + part
    ucon[:, nu + E + NT * nu:] = S + _np.arange(NT)[None, :] * P + part
    icon = _np.zeros((P, BLK + 2), _np.float16)
    icon[:, 0:BLK] = _np.arange(BLK)
    step = _np.full(2 * P, P, _np.float16)
    step[::NB * NT] = -P * (NB * NT - 1)
    step[0] = 0
    icon[:, BLK:] = step.reshape(2, P).T
    given += [("consts", consts), ("ucon", ucon), ("icon", icon), ("inv", inv)]
    arrays, args = {}, []
    for name, a in given:
        arrays[f"in_{name}_dram"] = a
        args.append(nc.dram_tensor(f"in_{name}_dram", a.shape, _mybir.dt.from_np(a.dtype), kind="ExternalInput").ap())
    res = nc.dram_tensor("out_0_dram", (S + NPAD, D), _mybir.dt.float32, kind="ExternalOutput").ap()
    adaln_moe(nc, *args, res)
    r = _run(nc, [arrays], core_ids=[0])
    return _np.asarray(r.results[0]["out_0_dram"])[:S].reshape(2, SEQ, D)
```

```python
from contextlib import ExitStack

import numpy as np

import concourse.bass as bass
from concourse import mybir

ALU = mybir.AluOpType
ACT = mybir.ActivationFunctionType
F32 = mybir.dt.float32
F32R = mybir.dt.float32r
I32 = mybir.dt.int32
U32 = mybir.dt.uint32
F16 = mybir.dt.float16
AX_X = mybir.AxisListType.X

P = 128
D = 128
F = 512
E = 8
NC = F // P
S = 4096
SEQ = 2048
BLK = 512
NB = S // BLK
NT = BLK // P
TOPK = 2 * S
EPS = 1e-5

HEAD_STEPS = 16
UNIT0 = 44
RING = 6
NU = 2 * NB + E - 1
ROW = D + E + D
NPAD = BLK
CW = 2 * BLK
CW_END = (CW + 4 * BLK) // BLK
XR = 5
PACE = 6
UMIN = TOPK // BLK
TOPK_SLOT = 4 * (NB - 1) + HEAD_STEPS


class Lane:

    def __init__(self):
        self.items = []


class Marks:

    def __init__(self, new_sem):
        self.new_sem = new_sem
        self.sems = {}

    def raise_(self, name, n):
        if name not in self.sems:
            self.sems[name] = [self.new_sem("s_" + name), 0]
        s = self.sems[name]
        s[1] += n
        return name, s[1]


def adaln_moe(nc, x, gw, w1, b1, w2, b2, ws1, bs1, ws2, bs2, c_in, wmod, consts, ucon, icon, inv, out):
    rows_dram = nc.dram_tensor("rows_scratch", [S + NPAD, ROW], F32, kind="Internal").ap()

    with ExitStack() as ctx:
        def sb(name, shape, dt=F32):
            return ctx.enter_context(nc.sbuf_tensor(name, shape, dt))

        def ps(name):
            return ctx.enter_context(nc.psum_tensor(name, [P, BLK], F32))

        tag = [-1]
        marks = Marks(lambda n: ctx.enter_context(nc.semaphore(n)))
        lanes = {k: Lane() for k in ("sync", "scalar", "vector", "gpsimd", "tensor")}

        def put(lane, fn, after=(), mark=None, n=1):
            m = marks.raise_(mark, n) if mark else None
            lanes[lane].items.append((tuple(a for a in after if a), fn, m, n, tag[0]))
            return m

        def dma(lane, dst, src, mark, after=()):
            return put(lane, lambda e: e.dma_start(dst, src), after, mark, 16)

        W1h, W1l = sb("W1h", [P, E + 1, F], F32R), sb("W1l", [P, E + 1, F], F32R)
        W2h, W2l = sb("W2h", [P, E + 1, NC, D], F32R), sb("W2l", [P, E + 1, NC, D], F32R)
        H2h, H2l = sb("H2h", [P, S], F32R), sb("H2l", [P, S], F32R)
        ACC = sb("ACC", [P, S])
        HF = sb("HF", [P, 4, BLK])
        Hh, Hl = sb("Hh", [P, RING, BLK], F32R), sb("Hl", [P, RING, BLK], F32R)
        TMP = sb("TMP", [P, 2, BLK])
        OUT = sb("OUT", [P, 2, NT, P])
        HT = OUT
        R1 = sb("R1", [P, 8192])
        CST = sb("CST", [P, 3 * P])
        COL = sb("COL", [P, 64])
        SM = sb("SM", [P, 192])
        GWh, GWl = sb("GWh", [P, E], F32R), sb("GWl", [P, E], F32R)
        CNT = sb("CNT", [P, 2], F16)
        TR16 = sb("TR16", [P, P], F16)
        TIE = sb("TIE", [P, 256], F16)
        ON16 = sb("ON16", [P, P], F16)
        TI = sb("TI", [P, 4], I32)

        IDENT, TRI, ONES = CST[:, 0:P], CST[:, P:2 * P], CST[:, 2 * P:3 * P]
        XG = R1[:, 0:XR * NT * ROW].rearrange("p (k t c) -> p k t c", k=XR, t=NT)
        YE = R1[:, 5280:6304].rearrange("p (k s) -> p k s", k=2)
        YO = R1[:, 6304:7328].rearrange("p (k t c) -> p k t c", k=2, t=NT)
        WS = R1[:, 3072:5120].rearrange("p (k s) -> p k s", k=2)
        X = R1[:, 0:1536].rearrange("p (k t c) -> p k t c", k=3, t=NT)
        XN = R1[:, 1536:2560].rearrange("p (k t c) -> p k t c", k=2, t=NT)
        XN2 = R1[:, 2560:3072].rearrange("p (t c) -> p t c", t=NT)
        WMOD = R1[:, 5120:5888]
        ROWS = R1[0:64, 5888:6016]
        LR = R1[0:E, 5120:5632]
        CT = R1[:, 6144:7168].rearrange("p (k s) -> p k s", k=2)
        MT = R1[:, 7168:7680]
        INV = sb("INV", [P, 2, BLK])
        H2F = R1[:, 7680:8192]
        TK = R1[:, 6272:7808].rearrange("p (k s) -> p k s", k=6)
        tk = [TK[:, i, :] for i in range(6)]
        GBC = sb("GBC", [P, 2, D])
        UC = sb("UC", [P, NU + E + NT * NU + NT])
        IC = sb("IC", [P, BLK + 2], F16)
        UIOTA, E8 = UC[:, 0:NU], UC[:, NU:NU + E]
        SIG = UC[:, NU + E:NU + E + NT * NU]
        PADR = UC[:, NU + E + NT * NU:NU + E + NT * NU + NT]
        IOTA, DT = IC[:, 0:BLK], IC[:, BLK:BLK + 2]
        CMP = R1[:, 7808:7808 + NU * E].rearrange("p (u e) -> p u e", u=NU)
        OH = R1[:, 8000:8000 + NU * E].rearrange("p (u e) -> p u e", u=NU)
        EX8 = sb("EX8", [P, 6, E])
        EIDF = sb("EIDF", [P, NU])
        EIDI = sb("EIDI", [P, NU], I32)
        USED = sb("USED", [P, 1], I32)
        UTI = sb("UTI", [P, 2, E], I32)
        IDXB = sb("IDXB", [P, NU, NT], U32)
        STC = sb("STC", [P, 2])
        DQ = sb("DQ", [P, 2, P], F16)
        HM = INV[:, :, :].rearrange("p k s -> p (k s)").bitcast(F16).rearrange("p (k c s) -> p k c s", k=2, c=2)
        CNB = sb("CNB", [P, 4, NT])
        GJ = sb("GJ", [P, P])
        CB1, CB2 = sb("CB1", [P, 2, NC]), sb("CB2", [P, 3, 1])
        GTM, GT4 = sb("GTM", [P, NT, E]), sb("GT4", [P, 2, NT])
        SCT = R1[:, 5888:6144]

        UB = [ps("U0"), ps("U1")]
        YB = [ps("Y0"), ps("Y1")]
        RB = [ps("R0"), ps("R1b"), ps("R2")]
        LG = ps("LG")

        SIL = SM[:, 0:2]
        MOD = SM[:, 2:14]
        MODv = MOD.rearrange("p (h k) -> p h k", h=2)
        SGN = SM[:, 14:18].rearrange("p (h k) -> p h k", h=2)
        MX = SM[:, 18:22].rearrange("p (h k) -> p h k", h=2)
        GG = SM[:, 22:26].rearrange("p (h k) -> p h k", h=2)
        OP = SM[:, 26:30].rearrange("p (h k) -> p h k", h=2)
        CA = SM[:, 30:32]
        CB = SM[:, 32:34]
        GBS = SM[:, 34:36]
        NHALF = SM[:, 36:40]
        KR = SM[:, 40:41]
        ST = SM[:, 64:112].rearrange("p (k t s) -> p k t s", k=2, t=NT)
        MV = SM[:, 112:128].rearrange("p (k t s) -> p k t s", k=2, t=NT)
        VE = SM[:, 128:136].rearrange("p (k t) -> p k t", k=2)
        NM = SM[:, 184:192].rearrange("p (k t) -> p k t", k=2)
        RS = SM[:, 136:152].rearrange("p (k j t) -> p k j t", k=2, j=2)

        ld_cst = dma("sync", CST[:, :], consts, "ld_cst")
        b1r = b1.rearrange("e (c p) -> (e c) p", p=P)
        dma("sync", UC[:, :], ucon, "ld_uc")
        ld_uc = dma("sync", IC[:, :], icon, "ld_uc")
        ld_rows = None
        for dst, src in ((ROWS[0:32, :], b1r), (ROWS[32:36, :], bs1.rearrange("(c p) -> c p", p=P)),
                         (ROWS[36:44, :], b2), (ROWS[44:45, :], bs2.rearrange("(a p) -> a p", a=1)),
                         (ROWS[45:47, :], c_in), (ROWS[47:55, :], gw)):
            ld_rows = dma("scalar", dst, src, "ld_rows")

        x_used = {}

        def load_x(b):
            src = x[b * BLK:(b + 1) * BLK, :].rearrange("(t p) c -> p t c", p=P)
            return dma("sync", X[:, b % 3, :, :], src, f"ld_x{b % 3}", [x_used.get(b - 3)])

        ld_x = {0: load_x(0)}
        ld_wmod = dma("scalar", WMOD, wmod, "ld_wmod")
        ld_x[1] = load_x(1)

        w_used = {}
        ld_w = {}

        def load_w(j):
            k = WORDER.index(j) % 2
            s1 = ws1 if j == E else w1[j]
            s2 = (ws2 if j == E else w2[j]).rearrange("(c p) d -> p c d", p=P)
            free = w_used.get(k, ())
            dma("sync", WS[:, k, 0:F], s1, f"ld_w{k}", free)
            ld_w[j] = dma("sync", WS[:, k, F:2 * F].rearrange("p (c d) -> p c d", c=NC), s2, f"ld_w{k}")

        WORDER = [E] + list(range(E))
        inv_used = {}
        ld_inv = {}

        def load_inv(b):
            q = b % 4
            src = inv[0, q * BLK:(q + 1) * BLK].partition_broadcast(P)
            ld_inv[b] = dma("sync", INV[:, b % 2, :], src, f"ld_inv{b % 2}", [inv_used.get(b - 2)])

        load_w(E)
        load_inv(0)
        load_inv(1)
        ld_x[2] = load_x(2)
        load_w(0)

        tr16 = put("gpsimd", lambda e: e.tensor_copy(TR16[:, :], TRI), [ld_cst], "on16")
        on16 = put("gpsimd", lambda e: e.memset(ON16[:, :], 1.0), mark="on16")
        nhalf = put("gpsimd", lambda e: e.memset(NHALF, -0.5), mark="nhalf")

        HB = RB + YB
        free_banks = [(k, None) for k in (range(5) if UNIT0 >= 4 * NB else range(3))]

        def give_bank(k, mark):
            free_banks.append((k, mark))

        def take_bank():
            k, mark = free_banks.pop(0)
            return k, HB[k], mark

        kb, bank, free = take_bank()
        m = put("tensor", lambda e, bank=bank: e.transpose(bank[:, 0:55], ROWS[0:55, :], IDENT[0:55, 0:55]),
                [ld_cst, ld_rows], "pe_cols")
        cols = put("vector", lambda e, bank=bank: e.tensor_copy(COL[:, 0:55], bank[:, 0:55]), [m], "v_cols")
        give_bank(kb, cols)
        B1, B2, GWC = COL[:, 0:36], COL[:, 36:45], COL[:, 47:55]
        sil = put("scalar", lambda e: e.activation(SIL, COL[:, 45:47], ACT.Silu), [cols], "a_sil")
        gwh = put("vector", lambda e: e.tensor_copy(GWh[:, :], GWC), [cols], "v_gw")
        gwl = put("vector", lambda e: e.tensor_tensor(GWl[:, :], GWC, GWh[:, :].bitcast(F32), ALU.subtract),
                  [gwh], "v_gw")
        kb, bank, free = take_bank()
        for j in range(6):
            m = put("tensor", lambda e, j=j, bank=bank: e.matmul(
                bank[:, 2 * j:2 * j + 2], WMOD[:, j * P:(j + 1) * P], SIL, start=True, stop=True),
                [sil, ld_wmod], "pe_mod")
        mod = put("vector", lambda e, bank=bank: e.tensor_copy(MOD, bank[:, 0:12]), [m], "v_mod")
        give_bank(kb, mod)
        sgn = put("vector", lambda e: e.tensor_scalar(SGN, MODv[:, :, 4:6], 0.0, 2.0, ALU.is_ge, ALU.mult),
                  [mod], "v_mod")
        pm = put("vector", lambda e: e.tensor_scalar(SGN, SGN, 1.0, None, ALU.subtract), [sgn], "v_mod")
        mxa = put("vector", lambda e: e.tensor_tensor(MX, SGN, MODv[:, :, 4:6], ALU.mult), [pm], "v_mod")
        onep = put("vector", lambda e: e.tensor_scalar(OP, MODv[:, :, 2:4], 1.0, None, ALU.add), [mod], "v_mod")
        gg = put("vector", lambda e: e.scalar_tensor_tensor(GG, MX, 0.25, SGN, ALU.max, ALU.mult), [mxa], "v_mod")
        ca = put("vector", lambda e: e.tensor_tensor(CA, GG[:, 0, :], OP[:, 0, :], ALU.mult), [gg, onep], "v_mod")
        cbm = put("vector", lambda e: e.tensor_tensor(CB, GG[:, 0, :], MODv[:, 0, 0:2], ALU.mult), [gg], "v_mod")
        modv = put("vector", lambda e: e.tensor_scalar(GBS, GG[:, 1, :], B2[:, 8:9], None, ALU.mult),
                   [gg], "v_mod")
        gbd = []
        for n in range(2):
            gbd.append(put("vector", lambda e, n=n: e.tensor_scalar(TMP[:, 0, n * P:(n + 1) * P], IDENT, GG[:, 1, n:n + 1],
                                                                  None, ALU.mult), [gg, ld_cst], "v_gbd"))
        kb, bank, free = take_bank()
        m = put("tensor", lambda e, bank=bank: e.matmul(bank[:, 0:2 * P], ONES, TMP[:, 0, 0:2 * P], start=True, stop=True),
                [gbd[1], free], "pe_gbc")
        gbc = put("vector", lambda e, bank=bank: e.tensor_copy(GBC[:, :, :].rearrange("p n c -> p (n c)"), bank[:, 0:2 * P]),
                  [m], "v_gbc")
        give_bank(kb, gbc)
        zero = put("vector", lambda e: e.memset(OUT[:, 0:2, :, :], 0.0), mark="v_zero")
        half = S // 2
        gb_rows = []
        for n in range(2):
            gb_rows.append(dma("sync", rows_dram[n * half:(n + 1) * half, D + E:ROW].rearrange("(t p) c -> p t c", p=P),
                GBC[:, n, :].unsqueeze(1).to_broadcast([P, half // P, D]), f"st_gb{n}", [gbc]))
        zrow = [dma("sync", out[S:S + NPAD, :].rearrange("(t p) c -> p t c", p=P), OUT[:, 0, :, :], "st_z0", [zero])]
        flat = OUT[:, :, :, :].rearrange("p k t c -> p (k t c)")
        for t in range(NT):
            zrow.append(dma("sync", rows_dram[S + t * P:S + (t + 1) * P, :], flat[:, 0:ROW], f"st_z{1 + t}", [zero]))
        C1, SB2, GBV = OP[:, 1, :], MODv[:, 1, 0:2], GG[:, 1, :]

        w_ready = {}

        def split_w(j, part, act, low):
            k = WORDER.index(j) % 2
            src = WS[:, k, part * F:(part + 1) * F]
            hi = (W1h[:, j, :] if part == 0 else W2h[:, j, :, :].rearrange("p c d -> p (c d)"))
            lo = (W1l[:, j, :] if part == 0 else W2l[:, j, :, :].rearrange("p c d -> p (c d)"))
            if act == "scalar":
                h = put(act, lambda e: e.activation(hi, src, ACT.Copy), [ld_w[j]], "a_w")
            else:
                h = put(act, lambda e: e.tensor_copy(hi, src), [ld_w[j]], "v_w")
            low_m = put(low, lambda e: e.tensor_tensor(lo, src, hi.bitcast(F32), ALU.subtract), [h],
                        {"vector": "v_wl", "gpsimd": "g_wl"}[low])
            w_ready[j, part] = (h, low_m)
            w_used[k] = w_used.get(k, ()) if part else ()
            w_used[k] = w_used[k] + (h, low_m)

        hd = {}
        ct_last = {}
        st_used = {}
        h2_ready = {}
        acc_ready = {}
        lg_ready = [None]
        xn_used = {}
        misc = {}
        ht_used = {}

        def stats(b, src, ready, tag):
            k = {"1": 0, "2": 1}[tag]
            m = None
            for t in range(NT):
                m = put("vector", lambda e, t=t: e.bn_stats(ST[:, k, t, :], src[:, t, :]),
                        [ready, st_used.get(("st", k))] if t == 0 else (), "v_st")
            for t in range(NT):
                a = put("vector", lambda e, t=t: e.bn_aggr(MV[:, k, t, :], ST[:, k, t, :]),
                        [m, st_used.get(("mv", k))] if t == 0 else (), "v_st")
            st_used["st", k] = a
            v = put("gpsimd", lambda e: e.tensor_scalar(VE[:, k, :], MV[:, k, :, 1], 1.0, EPS, ALU.mult, ALU.add),
                    [a], "g_rs")
            if tag == "2":
                g = put("gpsimd", lambda e: e.tensor_scalar(NM[:, k, :], MV[:, k, :, 0], -1.0, 0.0, ALU.mult, ALU.add),
                        [a], "g_rs")
            n = put("gpsimd", lambda e: e.tensor_tensor(RS[:, k, 0, :], VE[:, k, :], NHALF, ALU.pow),
                    [v, nhalf, st_used.get(("rs", k))], "g_rs")
            if tag == "2":
                n = put("gpsimd", lambda e: e.tensor_tensor(RS[:, k, 1, :], NM[:, k, :], RS[:, k, 0, :], ALU.mult),
                        [n, g], "g_rs")
            st_used["mv", k] = n
            return n

        def transposes(dst, src, after, mark):
            for t in range(NT):
                m = put("tensor", lambda e, t=t: e.transpose(dst(t), src(t), IDENT), after if t == 0 else (),
                        mark if t == NT - 1 else None)
            return m

        def head(b, s):
            n = b // 4
            q = hd.setdefault(b, {})
            xs = X[:, b % 3, :, :]
            if s == 0:
                q["nm"] = stats(b, xs, ld_x[b], "1")
            elif s == 2:
                for t in range(NT):
                    q["xn"] = put("vector", lambda e, t=t: e.tensor_scalar(
                        XN[:, b % 2, t, :], xs[:, t, :], MV[:, 0, t, 0:1], RS[:, 0, 0, t:t + 1],
                        ALU.subtract, ALU.mult), [q["nm"], xn_used.get(b - 2)], "v_xn")
                st_used["rs", 0] = st_used["mv", 0] = q["xn"]
            elif s == 3:
                k1, T1, f1 = take_bank()
                q["t1"] = transposes(lambda t: T1[:, t * P:(t + 1) * P], lambda t: XN[:, b % 2, t, :],
                                     [q["xn"], f1], "pe_t1")
                k2, T2, f2 = take_bank()
                q["t2"] = transposes(lambda t: T2[:, t * P:(t + 1) * P], lambda t: xs[:, t, :], [f2], "pe_t2")
                xn_used[b] = q["t1"]
                x_used[b] = q["t2"]
                q["T1"], q["T2"] = (k1, T1), (k2, T2)
                if b + 3 < NB:
                    ld_x[b + 3] = load_x(b + 3)
            elif s == 4:
                k1, T1 = q["T1"]
                k2, T2 = q["T2"]
                first = b % 4 == 0
                init = 0.0 if first else CT[:, (b - 1) % 2, BLK - 1:BLK]
                c = put("vector", lambda e: e.tensor_tensor_scan(
                    CT[:, b % 2, :], ONES[:, 0:1].to_broadcast([P, BLK]), T1[:, :], init, ALU.mult, ALU.add),
                    [q["t1"], ct_last.get(b - 1), ld_cst], "v_ct")
                ct_last[b] = c
                give_bank(k1, c)
                mm = put("vector", lambda e: e.scalar_tensor_tensor(
                    MT, CT[:, b % 2, :], CA[:, n:n + 1], INV[:, b % 2, :], ALU.mult, ALU.mult),
                    [c, ld_inv[b], modv, misc.get("mt")], "v_mt")
                inv_used[b] = mm
                if b + 2 < NB:
                    load_inv(b + 2)
                q["x2"] = put("vector", lambda e: e.scalar_tensor_tensor(
                    ACC[:, b * BLK:(b + 1) * BLK], T2[:, :], CB[:, n:n + 1], MT, ALU.add, ALU.add),
                    [mm, q["t2"]], "v_x2")
                misc["mt"] = q["x2"]
                give_bank(k2, q["x2"])
            elif s == 5:
                k3, T3, f3 = take_bank()
                q["t3"] = transposes(lambda t: T3[:, t * P:(t + 1) * P],
                                     lambda t: ACC[:, b * BLK + t * P:b * BLK + (t + 1) * P],
                                     [q["x2"], f3], "pe_t3")
                q["T3"] = (k3, T3)
                acc_ready[b] = q["t3"]
            elif s == 6:
                k3, T3 = q["T3"]
                q["nm2"] = stats(b, T3[:, :].rearrange("p (t c) -> p t c", t=NT), q["t3"], "2")
            elif s == 8:
                k3, T3 = q["T3"]
                for t in range(NT):
                    m = put("scalar", lambda e, t=t: e.activation(
                        XN2[:, t, :], T3[:, t * P:(t + 1) * P], ACT.Identity,
                        bias=RS[:, 1, 1, t:t + 1], scale=RS[:, 1, 0, t:t + 1]),
                        [q["nm2"], misc.get("xn2")], "a_xn2")
                q["xn2"] = m
                st_used["rs", 1] = m
                give_bank(k3, m)
            elif s == 9:
                k4, T4, f4 = take_bank()
                q["t4"] = transposes(lambda t: T4[:, t * P:(t + 1) * P], lambda t: XN2[:, t, :],
                                     [q["xn2"], f4], "pe_t4")
                misc["xn2"] = q["t4"]
                q["T4"] = (k4, T4)
            elif s == 10:
                k4, T4 = q["T4"]
                f = put("scalar", lambda e: e.activation(H2F, T4[:, :], ACT.Identity, bias=SB2[:, n:n + 1],
                                                         scale=C1[:, n:n + 1]),
                        [q["t4"], misc.get("h2l"), misc.get("h2h"), misc.get("h2t")], "a_h2f")
                give_bank(k4, f)
                h = put("scalar", lambda e: e.activation(H2h[:, b * BLK:(b + 1) * BLK], H2F, ACT.Copy), [f], "a_h2")
                q["h2h"] = h
            elif s == 11:
                h = q["h2h"]
                lo = put("vector", lambda e: e.tensor_tensor(
                    H2l[:, b * BLK:(b + 1) * BLK], H2F, H2h[:, b * BLK:(b + 1) * BLK].bitcast(F32), ALU.subtract),
                    [h], "v_h2l")
                misc["h2l"], misc["h2h"] = lo, h
                h2_ready[b] = (h, lo)
            elif s == 12:
                k6, T6, f6 = take_bank()
                q["t6"] = transposes(lambda t: T6[:, t * P:(t + 1) * P], lambda t: H2F[:, t * P:(t + 1) * P],
                                     [q["h2h"], f6], "pe_t6")
                q["T6"] = (k6, T6)
                misc["h2t"] = q["t6"]
            elif s == 13:
                k6, T6 = q["T6"]
                m = put("scalar", lambda e: e.activation(HT[:, b % 2, :, :].rearrange("p t c -> p (t c)"), T6[:, :],
                                                         ACT.Copy), [q["t6"], *([ht_used[b - 2]] if b >= 2 else zrow)], "a_ht")
                give_bank(k6, m)
                ht_used[b] = dma("sync", rows_dram[b * BLK:(b + 1) * BLK, 0:D].rearrange("(t p) c -> p t c", p=P),
                                 HT[:, b % 2, :, :], f"st_ht{b % 2}", [m])
            elif s == 14:
                k5, T5, f5 = take_bank()
                hs, ls = H2h[:, b * BLK:(b + 1) * BLK], H2l[:, b * BLK:(b + 1) * BLK]
                for i, (a, r) in enumerate(((GWh, hs), (GWh, ls), (GWl, hs))):
                    m = put("tensor", lambda e, a=a, r=r, i=i: e.matmul(
                        T5[0:E, :], a[:, :], r, start=i == 0, stop=i == 2),
                        [*h2_ready[b], gwl, f5] if i == 0 else (), "pe_lr" if i == 2 else None)
                q["lr"], q["T5"] = m, (k5, T5)
            elif s == 15:
                k5, T5 = q["T5"]
                m = put("scalar", lambda e: e.activation(LR, T5[0:E, :], ACT.Copy),
                        [q["lr"], misc.get("lrt"), mod], "a_lr")
                give_bank(k5, m)
                for t in range(NT):
                    j = (b * NT + t) * E
                    mt = put("tensor", lambda e, t=t, j=j: e.transpose(
                        LG[:, j:j + E], LR[:, t * P:(t + 1) * P], IDENT[0:E, 0:E]), [m],
                        "pe_lg" if t == NT - 1 else None)
                misc["lrt"] = mt
                lg_ready[0] = mt

        units = [(E, b) for b in range(NB)] + [(None, v) for v in range(NU)]
        gelu, cast, low, h_used = {}, {}, {}, {}
        up_done = {}
        u_read = [None, None]
        y_read = [None, None]
        y_done = {}
        xt_ready = {}
        cw1_ready, cw2_ready = {}, {}
        CWS = [H2h[:, CW:CW + 4 * BLK], H2l[:, CW:CW + 4 * BLK]]

        def up(g):
            u = g // NC
            j, b = units[u]
            c = g % NC
            bank = UB[g % 2]
            if u < NB:
                wh, wl = W1h[:, j, c * P:(c + 1) * P], W1l[:, j, c * P:(c + 1) * P]
                hs, ls = H2h[:, b * BLK:(b + 1) * BLK], H2l[:, b * BLK:(b + 1) * BLK]
                bias = B1[:, j * NC + c:j * NC + c + 1]
                need = [*h2_ready[b], *w_ready[j, 0]]
            else:
                k = b % 2
                wh, wl = CWS[k][:, c * P:(c + 1) * P], CWS[k][:, BLK + c * P:BLK + (c + 1) * P]
                hs, ls = H2h[:, k * BLK:(k + 1) * BLK], H2l[:, k * BLK:(k + 1) * BLK]
                bias = CB1[:, k, c:c + 1]
                need = [*xt_ready[b], *cw1_ready[b]]
            for i, (a, r) in enumerate(((wh, hs), (wh, ls), (wl, hs))):
                m = put("tensor", lambda e, a=a, r=r, i=i: e.matmul(bank[:, :], a, r, start=i == 0, stop=i == 2),
                        [*need, u_read[g % 2]] if i == 0 else (), "pe_up" if i == 2 else None)
            up_done[g] = m
            gelu[g] = put("scalar", lambda e: e.activation(HF[:, g % 4, :], bank[:, :], ACT.Gelu_apprx_tanh, bias=bias),
                          [m, low.get(g - 4), cast.get(g - 4), cols], "a_gelu")
            u_read[g % 2] = gelu[g]

        def cast_h(g):
            hi, src = Hh[:, g % RING, :], HF[:, g % 4, :]
            if g % NC == 1:
                cast[g] = put("vector", lambda e: e.tensor_copy(hi, src), [gelu[g], h_used.get(g - RING)], "v_cast")
            else:
                cast[g] = put("scalar", lambda e: e.activation(hi, src, ACT.Copy),
                              [gelu[g], h_used.get(g - RING)], "a_cast")

        def low_h(g):
            hi, lo, src = Hh[:, g % RING, :], Hl[:, g % RING, :], HF[:, g % 4, :]
            lane = "gpsimd" if g < NC * NB and g % NC in (0,2) else "vector"
            low[g] = put(lane, lambda e: e.tensor_tensor(lo, src, hi.bitcast(F32), ALU.subtract),
                         [cast[g], h_used.get(g - RING)], {"vector": "v_low", "gpsimd": "g_low"}[lane])

        def down(g):
            u = g // NC
            j, b = units[u]
            c = g % NC
            bank = YB[u % 2]
            if u < NB:
                wh, wl = W2h[:, j, c, :], W2l[:, j, c, :]
                need = w_ready[j, 1]
            else:
                w = CWS[b % 2]
                wh, wl = w[:, 2 * BLK + c * P:2 * BLK + (c + 1) * P], w[:, 3 * BLK + c * P:3 * BLK + (c + 1) * P]
                need = cw2_ready[b]
            hi, lo = Hh[:, g % RING, :], Hl[:, g % RING, :]
            for i, (a, r) in enumerate(((wh, hi), (wh, lo), (wl, hi))):
                m = put("tensor", lambda e, a=a, r=r, i=i: e.matmul(
                    bank[:, :], a, r, start=(c == 0 and i == 0), stop=(c == NC - 1 and i == 2)),
                    [cast[g], low[g], *need, y_read[u % 2] if c == 0 else None] if i == 0 else (),
                    "pe_dn" if i == 2 else None)
            h_used[g] = m
            if c == NC - 1:
                y_done[u] = m

        tmp_used = [None, None]
        tmp_next = [0]
        out_free = [None, None]
        shared_done = {}
        stored = []

        def finish_shared(u):
            b = units[u][1]
            n = b // 4
            bank = YB[u % 2]
            k = tmp_next[0] % 2
            tmp_next[0] += 1
            a = put("scalar", lambda e: e.activation(TMP[:, k, :], bank[:, :], ACT.Identity,
                                                     bias=GBS[:, n:n + 1], scale=GBV[:, n:n + 1]),
                    [y_done[u], tmp_used[k], modv, gbc], "a_sh")
            y_read[u % 2] = a
            acc = ACC[:, b * BLK:(b + 1) * BLK]
            tmp_used[k] = shared_done[b] = put(
                "gpsimd", lambda e: e.tensor_tensor(acc, acc, TMP[:, k, :], ALU.add), [a, acc_ready[b]], "g_sh")

        def close(b):
            k, bank, free = take_bank()
            m = transposes(lambda t: bank[:, t * P:(t + 1) * P],
                           lambda t: ACC[:, b * BLK + t * P:b * BLK + (t + 1) * P], [shared_done[b], free], "pe_out")
            o = put("scalar", lambda e: e.activation(OUT[:, b % 2, :, :].rearrange("p t c -> p (t c)"), bank[:, :],
                                                     ACT.Copy), [m, out_free[b % 2] or ht_used[NB - 2 + b % 2]], "a_out")
            give_bank(k, o)
            dst = out[b * BLK:(b + 1) * BLK, :].rearrange("(t p) c -> p t c", p=P)
            out_free[b % 2] = dma("sync", dst, OUT[:, b % 2, :, :], f"st_out{b % 2}", [o])
            stored.append(out_free[b % 2])

        idx_ready, gathered, xt_done, yo_done, xl_of = {}, {}, {}, {}, {}
        ye_done, yt_done, scattered = {}, {}, {}
        hm_ready, g_done, g_read = {}, {}, {}
        reg = {}

        def idx_mask(v):
            for ch in range(2):
                m = put("vector", lambda e, ch=ch: e.tensor_scalar(
                    HM[:, v % 2, ch, :], IOTA, STC[:, ch:ch + 1], float(-BLK * v), ALU.subtract, ALU.is_ge),
                    [tkm["stc"], g_done.get(v - 2), ld_uc], "v_hm")
            hm_ready[v] = m

        def idx_mm(v):
            bank = RB[2]
            for s in range(NT):
                for ch in range(2):
                    lhs = HM[:, v % 2, ch, s * P:(s + 1) * P]
                    put("tensor", lambda e, s=s, ch=ch, lhs=lhs: e.matmul(
                        bank[:, s * P:(s + 1) * P], lhs, DQ[:, ch, :], start=ch == 0, stop=ch == 1),
                        [hm_ready[v], tkm["dq"], g_read.get(v - 1), *tkm["banks"]] if s == 0 and ch == 0 else ())
                for ch in range(2):
                    lhs = HM[:, v % 2, ch, s * P:(s + 1) * P]
                    m = put("tensor", lambda e, s=s, ch=ch, lhs=lhs: e.matmul(
                        LG[:, s:s + 1], lhs, DT[:, ch:ch + 1], start=ch == 0, stop=ch == 1),
                        (), "pe_idx" if s == NT - 1 and ch == 1 else None)
            g_done[v] = m

        def idx_count(v):
            bank = RB[2]
            c0, c1, c2, c3 = (CNB[:, i, :] for i in range(4))
            m = idx_ready.get(v - 1)
            for s in range(NT):
                i = NT * v + s
                m = put("vector", lambda e, s=s, i=i: e.tensor_scalar(
                    GJ[:, :], bank[:, s * P:(s + 1) * P], SIG[:, i:i + 1], None, ALU.is_le, ALU.add,
                    accum_out=c0[:, s:s + 1]), [g_done[v], m], "v_idx")
            a = put("vector", lambda e: e.tensor_tensor(c1, c0, LG[:, 0:NT], ALU.add), [m], "v_idx")
            g_read[v] = a
            b = put("vector", lambda e: e.tensor_tensor(c2, PADR, c1, ALU.subtract), [a], "v_idx")
            c = put("vector", lambda e: e.scalar_tensor_tensor(c3, c0, float(P), c2, ALU.is_ge, ALU.mult), [b], "v_idx")
            idx_ready[v] = put("vector", lambda e: e.tensor_tensor(IDXB[:, v, :], c1, c3, ALU.add), [c], "v_idx")

        def gather(v):
            for s in range(NT):
                m = put("gpsimd", lambda e, s=s: e.indirect_dma_start(
                    XG[:, v % XR, s, :], None, rows_dram, bass.IndirectOffsetOnAxis(ap=IDXB[:, v, s:s + 1], axis=0)),
                    [idx_ready[v], yo_done.get(v - XR), xt_done.get(v - XR), *tkm["rows"]], f"ld_xg{v % XR}", 16)
            gathered[v] = m

        def xt(v):
            bank = RB[0]
            xt_done[v] = transposes(lambda t: bank[:, t * P:(t + 1) * P], lambda t: XG[:, v % XR, t, 0:D],
                                    [gathered[v], *xl_of.get(v - 1, ()), *tkm["banks"]], "pe_xt")

        def split_x(v):
            bank = RB[0]
            k = v % 2
            hi, lo = H2h[:, k * BLK:(k + 1) * BLK], H2l[:, k * BLK:(k + 1) * BLK]
            free = [up_done[NC * (NB + v - 2) + NC - 1]] if v >= 2 else [up_done[NC * v + NC - 1], *h2_over]
            h = put("scalar", lambda e: e.activation(hi, bank[:, :], ACT.Copy), [xt_done[v], *free], "a_xh")
            lo_m = put("vector", lambda e: e.tensor_tensor(lo, bank[:, :], hi.bitcast(F32), ALU.subtract), [h, *free],
                       "v_xl")
            xl_of[v] = (h, lo_m)
            xt_ready[v] = (h, lo_m)

        def weights(v, part, lane, half):
            dst = CWS[v % 2][:, (2 * part + half) * BLK:(2 * part + half + 1) * BLK]
            src = ((W1h, W1l), (W2h, W2l))[part][half]
            if part == 0:
                src = src[:, :, :]
            else:
                src = src[:, :, :, :].rearrange("p e c d -> p e (c d)")
            src = src.bitcast(F32)
            free = up_done[CW_END * NC - 1]
            if v >= 2:
                free = up_done[NC * (NB + v - 2) + NC - 1] if part == 0 else h_used[NC * (NB + v - 2) + NC - 1]
            need = [tkm["eid"], free, *w_ready[E - 1, part], *(h2_over if v < 2 else ())]

            def fn(e, lane=lane):
                r = reg["vector", v] if lane == "vector" else e.value_load(EIDI[0:1, v:v + 1], min_val=0,
                                                                            max_val=E - 1)
                a = src[:, bass.ds(r, 1), :].rearrange("p a n -> p (a n)")
                return e.activation(dst, a, ACT.Copy) if lane == "scalar" else e.tensor_copy(dst, a)

            return put(lane, fn, need, {"scalar": "a_cw", "vector": "v_cw"}[lane] + str(part))

        def bias_cols(v):
            k = v % 2

            def fn1(e):
                reg["vector", v] = e.value_load(EIDI[0:1, v:v + 1], min_val=0, max_val=E - 1)
                a = B1[:, 0:E * NC].rearrange("p (e c) -> p e c", e=E)[:, bass.ds(reg["vector", v], 1), :]
                return e.tensor_copy(CB1[:, k, :], a.rearrange("p a n -> p (a n)"))

            def fn2(e):
                return e.tensor_copy(CB2[:, v % 3, :], B2[:, bass.ds(reg["vector", v], 1)])

            g = NC * (NB + v - 2) + NC - 1
            m = put("vector", fn1, [tkm["eid"], gelu.get(g) if v >= 2 else None], "v_cb")
            return m, put("vector", fn2, [ye_done.get(v - 3)], "v_cb")

        def weights_a(v):
            cb = bias_cols(v)
            cw1_ready[v] = [weights(v, 0, "scalar", 0), weights(v, 0, "vector", 1), *cb]

        def weights_b(v, half):
            cw2_ready.setdefault(v, []).append(weights(v, 1, "scalar", half))

        def ye(v):
            u = NB + v
            bank = YB[u % 2]
            ye_done[v] = put("scalar", lambda e: e.activation(YE[:, v % 2, :], bank[:, :], ACT.Identity,
                                                             bias=CB2[:, v % 3, :]),
                             [y_done[u], yt_done.get(v - 2), cw1_ready[v][3], *head_over], "a_ye")
            y_read[u % 2] = ye_done[v]

        def yt(v):
            bank = RB[1]
            yt_done[v] = transposes(lambda t: bank[:, t * P:(t + 1) * P], lambda t: YE[:, v % 2, t * P:(t + 1) * P],
                                    [ye_done[v], yo_done.get(v - 1), free_banks[0][1]], "pe_yt")

        def yo(v):
            bank = RB[1]
            k, r = v % 2, v % XR
            a = put("vector", lambda e: e.tensor_tensor(
                GTM[:, :, :], XG[:, r, :, D:D + E], OH[:, v, :].unsqueeze(1).to_broadcast([P, NT, E]), ALU.mult),
                [gathered[v], tkm["oh"], gt_last[0]], "v_gt")
            b = put("vector", lambda e: e.tensor_reduce(GT4[:, k, :], GTM[:, :, :], AX_X, ALU.add),
                    [a, yo_done.get(v - 2)], "v_gt")
            gt_last[0] = b
            for t in range(NT):
                m = put("vector", lambda e, t=t: e.scalar_tensor_tensor(
                    YO[:, k, t, :], bank[:, t * P:(t + 1) * P], GT4[:, k, t:t + 1], XG[:, r, t, D + E:ROW],
                    ALU.mult, ALU.mult), [b, yt_done[v], scattered.get(v - 2)], "v_yo")
            yo_done[v] = m

        gt_last = [None]

        def scatter(v):
            prev = scattered.get(v - 1)
            for s in range(NT):
                m = put("gpsimd", lambda e, s=s: e.indirect_dma_start(
                    out, bass.IndirectOffsetOnAxis(ap=IDXB[:, v, s:s + 1], axis=0), YO[:, v % 2, s, :], None,
                    compute_op=ALU.add, bounds_check=S + NPAD - 1, oob_is_err=True),
                    [yo_done[v], prev, *(stored[-2:] + zrow if v == 0 else ())], f"st_sc{v % 2}", 16)
            scattered[v] = m

        SC, EX, GT, EQ, CUMX, RK = tk
        SEL = EX
        SCv = SC.rearrange("p (e t) -> p e t", e=E)
        tkm = {}
        T_I, C_I, M_I = TI[:, 0:1], TI[:, 1:2], TI[:, 2:3]
        MXR, SMR, RCR = SM[:, 152:184], COL[:, 0:1], None
        RED = sb("RED", [P, 3, NB * NT])
        LGv = LG[:, 0:256].rearrange("p (t e) -> p t e", e=E)
        BITS = list(range(29, -1, -1))

        def tk_softmax(step):
            EXv = EX.rearrange("p (t e) -> p t e", e=E)
            if step == 0:
                a = put("vector", lambda e: e.tensor_reduce(RED[:, 0, :], LGv, AX_X, ALU.max), [lg_ready[0]], "v_tk")
                tkm["sub"] = put("vector", lambda e: e.tensor_tensor(
                    EXv, LGv, RED[:, 0, :].unsqueeze(2).to_broadcast([P, NB * NT, E]), ALU.subtract),
                    [a, *head_over], "v_tk")
                tkm["exp"] = put("scalar", lambda e: e.activation(EX, EX, ACT.Exp), [tkm["sub"]], "a_exp")
            else:
                a = put("vector", lambda e: e.tensor_reduce(RED[:, 1, :], EXv, AX_X, ALU.add), [tkm["exp"]], "v_tk")
                r = put("vector", lambda e: e.reciprocal(RED[:, 2, :], RED[:, 1, :]), [a], "v_tk")
                tkm["sc"] = put("vector", lambda e: e.tensor_tensor(
                    SCv.rearrange("p e t -> p t e"), EXv,
                    RED[:, 2, :].unsqueeze(2).to_broadcast([P, NB * NT, E]), ALU.mult), [r], "v_tk")
                t = put("gpsimd", lambda e: e.tensor_copy(SCT.rearrange("p (t e) -> p t e", e=E),
                                                          SCv.rearrange("p e t -> p t e")), [tkm["sc"]], "g_sct")
                st = dma("sync", rows_dram[0:S, D:D + E].rearrange("(t p) e -> p t e", p=P),
                         SCT.rearrange("p (t e) -> p t e", e=E), "st_sc", [t])
                tkm["rows"] = [st, *(ht_used[b] for b in (NB - 2, NB - 1)), *gb_rows, *zrow]
                z = put("vector", lambda e: e.memset(T_I, 0), mark="v_tk")
                tkm["t"] = z
                tkm["cand"] = put("vector", lambda e: e.memset(C_I, 1 << BITS[0]), mark="v_tk")

        def tk_count(i):
            tkm["cnt"] = put("vector", lambda e: e.tensor_scalar(
                GT, SC, C_I.bitcast(F32), None, ALU.is_ge, ALU.add, accum_out=CNT[:, i % 2:i % 2 + 1]),
                [tkm["sc"], tkm["cand"]], "v_cnt")

        def tk_sum(i):
            tkm["sum"] = put("tensor", lambda e: e.matmul(LG[:, 256 + i % 2:257 + i % 2], ON16[:, :],
                                                          CNT[:, i % 2:i % 2 + 1], start=True, stop=True),
                             [tkm["cnt"], on16], "pe_sum")

        def tk_step(i):
            bit = BITS[i]
            m = put("vector", lambda e: e.tensor_scalar(M_I, LG[:, 256 + i % 2:257 + i % 2], float(TOPK),
                                                        float(1 << bit), ALU.is_ge, ALU.mult),
                    [tkm["sum"], tkm["t"]], "v_tk")
            if bit:
                tkm["cand"] = put("vector", lambda e: e.scalar_tensor_tensor(
                    C_I, M_I, 1 << (bit - 1), T_I, ALU.bitwise_or, ALU.bitwise_or), [m, tkm["cnt"]], "v_cand")
            tkm["m"] = m
            if not bit:
                tk_keep()

        def tk_keep():
            tkm["t"] = put("vector", lambda e: e.tensor_tensor(T_I, T_I, M_I, ALU.bitwise_or),
                           [tkm["m"], tkm["t"], tkm["cand"]], "v_tk")

        def tk_bit(i):
            if 0 <= i < len(BITS):
                tk_sum(i)
                tk_step(i)
                if BITS[i]:
                    tk_count(i + 1)
                    tk_keep()

        def tk_ties(s):
            TF = T_I.bitcast(F32)
            if s == 0:
                a = put("vector", lambda e: e.tensor_scalar(GT, SC, TF, None, ALU.is_gt, ALU.add,
                                                            accum_out=CNT[:, 0:1]), [tkm["t"], tkm["cnt"]], "v_tk")
                q = put("vector", lambda e: e.tensor_scalar(TIE[:, :], SC, TF, None, ALU.is_equal), [tkm["t"]], "v_tk")
                tkm["masks"] = q
            elif s == 1:
                k, bank, free = take_bank()
                put("tensor", lambda e: e.matmul(LG[:, 260:261], ON16[:, :], CNT[:, 0:1], start=True, stop=True),
                    [tkm["masks"]])
                put("tensor", lambda e: e.matmul(bank[:, 0:256], TR16[:, :], TIE[:, :], start=True, stop=True), [free])
                m = put("tensor", lambda e: e.matmul(bank[:, 256:512], ON16[:, :], TIE[:, :], start=True, stop=True),
                        mark="pe_tie")
                r = put("vector", lambda e: e.tensor_scalar(KR, LG[:, 260:261], -1.0, float(TOPK), ALU.mult, ALU.add),
                        [m], "v_tk")
                c = put("vector", lambda e: e.tensor_tensor_scan(
                    CUMX, ONES[:, 0:1].to_broadcast([P, 256]), bank[:, 256:512], 0.0, ALU.mult, ALU.add), [m], "v_tk")
                c2 = put("vector", lambda e: e.tensor_tensor(RK, CUMX, bank[:, 256:512], ALU.subtract), [c], "v_tk")
                c3 = put("vector", lambda e: e.tensor_tensor(RK, RK, bank[:, 0:256], ALU.add), [c2], "v_tk")
                give_bank(k, c3)
                tkm["rk"] = c3
            elif s == 2:
                a = put("vector", lambda e: e.scalar_tensor_tensor(SEL, RK, KR, TIE[:, :], ALU.is_le, ALU.mult),
                        [tkm["rk"]], "v_tk")
                a = put("vector", lambda e: e.tensor_tensor(TIE[:, :], SEL, GT, ALU.add), [a], "v_tk")
                tkm["sel"] = a
            elif s == 3:
                k, bank, free = take_bank()
                put("tensor", lambda e: e.matmul(bank[:, 0:256], ON16[:, :], TIE[:, :], start=True, stop=True), [tkm["sel"], free])
                m = put("tensor", lambda e: e.matmul(bank[:, 256:512], TR16[:, :], TIE[:, :], start=True, stop=True), (), "pe_cum")
                TOT, CUM = bank[:, 0:256], bank[:, 256:512]
                NE, UT, UE, OFF = (EX8[:, i, :] for i in range(4))

                def v(fn, after):
                    return put("vector", fn, after, "v_ds")

                n = v(lambda e: e.tensor_reduce(NE, TOT.rearrange("p (e t) -> p e t", e=E), AX_X, ALU.add), [m])
                c = v(lambda e: e.tensor_tensor_scan(CUMX, ONES[:, 0:1].to_broadcast([P, 256]), TOT, 0.0,
                                                     ALU.mult, ALU.add), [n])
                n = v(lambda e: e.tensor_scalar(UTI[:, 0, :], NE, 1.0, float(BLK - 1), ALU.mult, ALU.add), [n])
                x_ = v(lambda e: e.tensor_tensor(RK, CUMX, TOT, ALU.subtract), [c])
                n = v(lambda e: e.tensor_scalar(UTI[:, 1, :], UTI[:, 0, :], 9, None, ALU.logical_shift_right), [n])
                n = v(lambda e: e.tensor_scalar(UT, UTI[:, 1, :], 1.0, None, ALU.max), [n])
                n = v(lambda e: e.tensor_tensor_scan(UE, ONES[:, 0:1].to_broadcast([P, E]), UT, 0.0,
                                                     ALU.mult, ALU.add), [n])
                tkm["used"] = v(lambda e: e.tensor_copy(USED[:, :], UE[:, E - 1:E]), [n])
                o = v(lambda e: e.tensor_tensor(OFF, UE, UT, ALU.subtract), [n])
                EXC0 = RK.rearrange("p (e t) -> p e t", e=E)[:, :, 0]
                o = v(lambda e: e.scalar_tensor_tensor(OFF, OFF, float(BLK), EXC0, ALU.mult, ALU.subtract), [o, x_])
                o = v(lambda e: e.tensor_tensor(GT.rearrange("p (e t) -> p e t", e=E),
                                                RK.rearrange("p (e t) -> p e t", e=E),
                                                OFF.unsqueeze(2).to_broadcast([P, E, NB * NT]), ALU.add), [o])
                q = v(lambda e: e.tensor_tensor(EQ, GT, CUM, ALU.add), [o])
                give_bank(k, q)
                q = v(lambda e: e.tensor_tensor(CUMX[:, 1:256], EQ[:, 1:256], EQ[:, 0:255], ALU.subtract), [q])
                q = v(lambda e: e.tensor_copy(CUMX[:, 0:1], EQ[:, 0:1]), [q])
                tkm["dqf"], tkm["start"] = q, o
            elif s == 4:
                k, bank, free = take_bank()
                for h in range(2):
                    put("tensor", lambda e, h=h: e.transpose(bank[:, h * P:(h + 1) * P],
                                                             CUMX[:, h * P:(h + 1) * P], IDENT),
                        [tkm["dqf"], tkm["start"], free])
                for h in range(2):
                    m = put("tensor", lambda e, h=h: e.transpose(bank[:, (2 + h) * P:(3 + h) * P],
                                                                 GT[:, h * P:(h + 1) * P], IDENT), (), "pe_dq")
                tkm["stc"] = put("vector", lambda e: e.tensor_copy(
                    STC[:, :], bank[:, 256:512].rearrange("p (k q) -> p k q", k=2)[:, :, 0]), [m], "v_ds")
                c = put("scalar", lambda e: e.activation(DQ[:, :, :].rearrange("p k q -> p (k q)"), bank[:, 0:256],
                                                         ACT.Copy), [tkm["stc"]], "a_dq")
                tkm["dq"] = c
                give_bank(k, c)
                tkm["banks"] = [mk for k, mk in free_banks if k != 1]
                free_banks[:] = [f for f in free_banks if f[0] == 1]
                idx_mask(0)
                UE = EX8[:, 2, :]
                a = put("vector", lambda e: e.tensor_tensor(
                    CMP[:, :, :], UE.unsqueeze(1).to_broadcast([P, NU, E]),
                    UIOTA.unsqueeze(2).to_broadcast([P, NU, E]), ALU.is_le), [tkm["start"], ld_uc], "v_eid")
                a = put("vector", lambda e: e.tensor_reduce(EIDF[:, :], CMP[:, :, :], AX_X, ALU.add), [a], "v_eid")
                a = put("vector", lambda e: e.tensor_scalar(EIDF[:, :], EIDF[:, :], float(E - 1), None, ALU.min),
                        [a], "v_eid")
                tkm["eid"] = put("vector", lambda e: e.tensor_copy(EIDI[:, :], EIDF[:, :]), [a], "v_eid")
                idx_mm(0)
                idx_count(0)
                gather(0)
                tkm["oh"] = put("vector", lambda e: e.tensor_tensor(
                    OH[:, :, :], EIDF[:, :].unsqueeze(2).to_broadcast([P, NU, E]),
                    E8.unsqueeze(1).to_broadcast([P, NU, E]), ALU.is_equal), [a], "v_eid")
            elif s == 5:
                idx_mask(1)
            elif s == 6:
                idx_mm(1)
                idx_mask(2)
                idx_count(1)
                gather(1)
            elif s == 7:
                idx_mm(2)
                idx_count(2)
                gather(2)
            if s == CW_STEP:
                weights_a(0)
            if s == XT_STEP:
                xt(0)
                split_x(0)

        bit_at = {2 * (TOPK_SLOT + 2) + i * PACE // 4: i for i in range(len(BITS))}
        tie0 = max(bit_at) // 2 + 1
        XT_STEP = max(UNIT0 + NC * NB - 1 - tie0, 7)
        CW_STEP = max(UNIT0 + NC * CW_END - tie0, 5)
        UNIT1 = tie0 + XT_STEP + 1
        NG = NC * len(units)
        GS = {UNIT0 + g: g for g in range(NC * NB)}
        GS.update({UNIT1 + g - NC * NB: g for g in range(NC * NB, NG)})
        head_over = []
        h2_over = []
        split_w(E, 0, "scalar", "vector")

        def run(stage, v, *more):
            if 0 <= v < NU:
                tag[0] = v
                stage(v, *more)
                tag[0] = -1

        def on_g(stage, s):
            if s in GS:
                tag[0] = GS[s] // NC - NB
                stage(GS[s])
                tag[0] = -1

        for s in range(UNIT1 + NC * (NU + 4)):
            if s == UNIT0 and UNIT0 >= 4 * NB:
                for k, mark in [f for f in free_banks if f[0] >= 3]:
                    y_read[k - 3] = mark
                    free_banks.remove((k, mark))
            on_g(up, s)
            on_g(cast_h, s - 1)
            on_g(low_h, s - 2)
            for b in range(NB):
                if 0 <= s - 4 * b < HEAD_STEPS:
                    head(b, s - 4 * b)
            if s == 1:
                split_w(E, 1, "scalar", "vector")
            if s % 3 == 2 and s // 3 < 2 * E:
                j, part = s // 3 // 2, s // 3 % 2
                if part == 0 and j + 1 < E:
                    load_w(j + 1)
                split_w(j, part, "scalar", "gpsimd")
            if s == TOPK_SLOT:
                q = hd[NB - 1]
                head_over = [q["t4"], misc["h2l"], misc["h2h"], misc["h2t"], lg_ready[0]]
                h2_over = [lg_ready[0], misc["lrt"], hd[NB - 1]["lr"]]
                tk_softmax(0)
            if s == TOPK_SLOT + 1:
                tk_softmax(1)
                tk_count(0)
            if 2 * s in bit_at:
                tk_bit(bit_at[2 * s])
            if s - 4 in GS and GS[s - 4] < NC * NB:
                g = GS[s - 4]
                down(g)
                if g % NC == NC - 1:
                    finish_shared(g // NC)
            if s - 6 in GS and GS[s - 6] % NC == NC - 1 and GS[s - 6] < NC * NB:
                close(GS[s - 6] // NC)
            if 0 <= s - tie0 <= XT_STEP:
                tk_ties(s - tie0)
            if 2 * s + 1 in bit_at:
                tk_bit(bit_at[2 * s + 1])
            v, c = (s - UNIT1) // NC, (s - UNIT1) % NC
            if v >= 0:
                if c == 0:
                    run(ye, v - 2)
                    run(weights_a, v + 1)
                    run(idx_mask, v + 3)
                elif c == 1:
                    run(xt, v + 1)
                    run(split_x, v + 1)
                    run(yt, v - 2)
                    run(idx_mm, v + 3)
                elif c == 2:
                    run(yo, v - 2)
                    run(scatter, v - 2)
                    run(weights_b, v, 0)
                elif c == 3:
                    run(weights_b, v, 1)
                    run(idx_count, v + 3)
                    run(gather, v + 3)
                if s - 4 in GS and GS[s - 4] >= NC * NB:
                    on_g(down, s - 4)

        block = ctx.enter_context(nc.Block())

        def emit(eng, lane):
            seen = {}
            used = None
            items = lanes[lane].items
            i = 0

            def wait(known, mark):
                name, value = mark
                if known.get(name, 0) < value:
                    eng.wait_ge(marks.sems[name][0], value)
                    known[name] = value

            def issue(known, item):
                after, fn, m, n, _ = item
                for a in after:
                    wait(known, a)
                ins = fn(eng)
                if m:
                    ins.then_inc(marks.sems[m[0]][0], n)

            while i < len(items):
                u = items[i][4]
                if u < UMIN:
                    issue(seen, items[i])
                    i += 1
                    continue
                if used is None:
                    wait(seen, tkm["used"])
                    used = eng.value_load(USED[0:1, 0:1], min_val=UMIN, max_val=NU)
                known = dict(seen)
                with eng.If(used > u):
                    while i < len(items) and items[i][4] == u:
                        issue(known, items[i])
                        i += 1
            return used

        @block.sync
        def _(eng):
            emit(eng, "sync")

        @block.scalar
        def _(eng):
            emit(eng, "scalar")

        @block.vector
        def _(eng):
            emit(eng, "vector")

        @block.gpsimd
        def _(eng):
            used = emit(eng, "gpsimd")
            for v in range(UMIN - 1, NU):
                name, value = scattered[v]
                if v < UMIN:
                    eng.wait_ge(marks.sems[name][0], value)
                else:
                    with eng.If(used > v):
                        eng.wait_ge(marks.sems[name][0], value)

        @block.tensor
        def _(eng):
            emit(eng, "tensor")


_INS = ["L0_attn_x", "L0_ffn_gate_weight", "L0_ffn_W1", "L0_ffn_b1", "L0_ffn_W2", "L0_ffn_b2",
        "L0_ffn_Ws1", "L0_ffn_bs1", "L0_ffn_Ws2", "L0_ffn_bs2", "L0_c", "L0_wmod"]


def kernel(**inputs):
    import numpy as _np
    import concourse.bacc as _bacc
    from concourse import mybir as _mybir
    from concourse.bass_utils import run_bass_kernel_spmd as _run

    nc = _bacc.Bacc("TRN2", target_bir_lowering=False, num_devices=1)
    eye = _np.eye(P, dtype=_np.float32)
    tri = _np.triu(_np.ones((P, P), _np.float32))
    consts = _np.concatenate([eye, tri, _np.ones((P, P), _np.float32)], axis=1)
    inv = (1.0 / _np.arange(1, SEQ + 1, dtype=_np.float64)).astype(_np.float32)[None, :]
    given = [(name, _np.ascontiguousarray(inputs[name])) for name in _INS]
    given[0] = (given[0][0], given[0][1].reshape(S, D))
    nu = NU
    ucon = _np.zeros((P, nu + E + NT * nu + NT), _np.float32)
    ucon[:, 0:nu] = _np.arange(nu)
    ucon[:, nu:nu + E] = _np.arange(E)
    part = _np.arange(P)[:, None]
    ucon[:, nu + E:nu + E + NT * nu] = _np.arange(NT * nu)[None, :] * P + part
    ucon[:, nu + E + NT * nu:] = S + _np.arange(NT)[None, :] * P + part
    icon = _np.zeros((P, BLK + 2), _np.float16)
    icon[:, 0:BLK] = _np.arange(BLK)
    step = _np.full(2 * P, P, _np.float16)
    step[::NB * NT] = -P * (NB * NT - 1)
    step[0] = 0
    icon[:, BLK:] = step.reshape(2, P).T
    given += [("consts", consts), ("ucon", ucon), ("icon", icon), ("inv", inv)]
    arrays, args = {}, []
    for name, a in given:
        arrays[f"in_{name}_dram"] = a
        args.append(nc.dram_tensor(f"in_{name}_dram", a.shape, _mybir.dt.from_np(a.dtype), kind="ExternalInput").ap())
    res = nc.dram_tensor("out_0_dram", (S + NPAD, D), _mybir.dt.float32, kind="ExternalOutput").ap()
    adaln_moe(nc, *args, res)
    r = _run(nc, [arrays], core_ids=[0])
    return _np.asarray(r.results[0]["out_0_dram"])[:S].reshape(2, SEQ, D)
```
